# Optimizing a Trainium2 kernel written in Bass

```python
import numpy as np
import jax
import jax.numpy as jnp

def _softmax(x, axis=-1):
    return jax.nn.softmax(x, axis=axis)

def _gelu(x):
    return jax.nn.gelu(x, approximate=True)

def _silu(x):
    return jax.nn.silu(x)

def _sigmoid(x):
    return jax.nn.sigmoid(x)

def _layernorm(x, axis=-1, eps=1e-05):
    m = jnp.mean(x, axis=axis, keepdims=True)
    v = jnp.var(x, axis=axis, keepdims=True)
    return (x - m) / jnp.sqrt(v + eps)

def _scatter_add(tgt, idx, src, axis=0):
    return tgt.at[idx].add(src)

def _segment_sum(src, seg, n):
    return jax.ops.segment_sum(src, seg, n)
kernel_name = 'mk_gnn_ffn_d1_gnn_r8_d63fe3'

def setup_inputs(seed: int=0):
    np.random.seed(seed)
    _w = jnp.asarray

    def _rec_inputs():
        import jax
        import jax.numpy as jnp
        _gk = jax.random.key(seed)
        x = -0.0003713 + 1 * jax.random.normal(jax.random.fold_in(_gk, 1), (6250, 256), jnp.float32)
        src = jax.random.randint(jax.random.fold_in(_gk, 2), (200000,), 0, 6250, jnp.int32)
        dst = jax.random.randint(jax.random.fold_in(_gk, 3), (200000,), 0, 6250, jnp.int32)
        _o = jnp.argsort(dst, stable=True)
        src = src[_o]
        dst = dst[_o]
        return (x, src, dst)
    x, src, dst = _rec_inputs()

    def _L0_gnn_setup():
        import jax, jax.numpy as jnp
        import numpy as np
        N, IN_CH, HEADS, OUT_CH, E = (6250, 256, 4, 64, 100000)
        key = jax.random.key(seed)
        k1, k2, k3, k4, k5 = jax.random.split(key, 5)
        x = jax.random.normal(k1, (N, IN_CH), dtype=jnp.float32)
        edge_index = jax.random.randint(k2, (2, E), 0, N, dtype=jnp.int64)
        bw = float(np.sqrt(6.0 / (IN_CH + HEADS * OUT_CH)))
        ba = float(np.sqrt(6.0 / (HEADS + OUT_CH)))
        weight = jax.random.uniform(k3, (IN_CH, HEADS * OUT_CH), jnp.float32, -bw, bw)
        attn_l = jax.random.uniform(k4, (HEADS, OUT_CH), jnp.float32, -ba, ba)
        attn_r = jax.random.uniform(k5, (HEADS, OUT_CH), jnp.float32, -ba, ba)
        return {'x': x, 'edge_index': edge_index, 'weight': weight, 'attn_l': attn_l, 'attn_r': attn_r}
    _L0_gnn_all = _L0_gnn_setup()
    _L0_gnn_in = {k: v for k, v in _L0_gnn_all.items() if k in ('weight', 'attn_l', 'attn_r')}
    del _L0_gnn_all

    def _L0_ffn_setup():
        import jax, jax.numpy as jnp
        import numpy as np
        B, T, D, H, E = (16, 512, 256, 512, 8)
        key = jax.random.key(seed)
        ks = jax.random.split(key, 5)
        x = jax.random.normal(ks[0], (B, T, D), dtype=jnp.float32)
        gate_w = jax.random.normal(ks[1], (D, E), dtype=jnp.float32) * 0.02
        gate_b = jnp.zeros((E,), dtype=jnp.float32)
        W1 = jax.random.normal(ks[2], (E, D, H), dtype=jnp.float32) * 0.02
        b1 = jnp.zeros((E, H), dtype=jnp.float32)
        W2 = jax.random.normal(ks[3], (E, H, D), dtype=jnp.float32) * 0.02
        b2 = jnp.zeros((E, D), dtype=jnp.float32)
        return {'x': x, 'gate_w': gate_w, 'gate_b': gate_b, 'W1': W1, 'b1': b1, 'W2': W2, 'b2': b2}
    _L0_ffn_all = _L0_ffn_setup()
    _L0_ffn_in = {k: v for k, v in _L0_ffn_all.items() if k in ('gate_w', 'gate_b', 'W1', 'b1', 'W2', 'b2')}
    del _L0_ffn_all
    return {'x': x, 'src': src, 'dst': dst, 'L0_gnn_weight': _L0_gnn_in['weight'], 'L0_gnn_attn_l': _L0_gnn_in['attn_l'], 'L0_gnn_attn_r': _L0_gnn_in['attn_r'], 'L0_ffn_gate_w': _L0_ffn_in['gate_w'], 'L0_ffn_gate_b': _L0_ffn_in['gate_b'], 'L0_ffn_W1': _L0_ffn_in['W1'], 'L0_ffn_b1': _L0_ffn_in['b1'], 'L0_ffn_W2': _L0_ffn_in['W2'], 'L0_ffn_b2': _L0_ffn_in['b2']}

def reference(x, src, dst, L0_gnn_weight, L0_gnn_attn_l, L0_gnn_attn_r, L0_ffn_gate_w, L0_ffn_gate_b, L0_ffn_W1, L0_ffn_b1, L0_ffn_W2, L0_ffn_b2):
    import jax
    import jax.numpy as jnp

    def _L0_gnn_ref(x, edge_index, weight, attn_l, attn_r):
        import jax, jax.numpy as jnp
        import numpy as np
        N, IN_CH, HEADS, OUT_CH, E = (6250, 256, 4, 64, 100000)
        heads, out_ch = attn_l.shape
        n = x.shape[0]
        xt = jnp.matmul(x, weight).reshape(-1, heads, out_ch)
        row, col = (edge_index[0], edge_index[1])
        alpha_l = jnp.einsum('ehd,hd->eh', xt[row], attn_l)
        alpha_r = jnp.einsum('ehd,hd->eh', xt[col], attn_r)
        alpha = jax.nn.softmax(jax.nn.leaky_relu(alpha_l + alpha_r, 0.01), axis=1)
        tmp = jnp.einsum('nh,nhd->nd', alpha[:n], xt[col[:n]])
        out = jnp.broadcast_to(tmp[:, None, :], (n, heads, out_ch))
        return out.reshape(n, heads * out_ch)

    def _L0_ffn_ref(x, gate_w, gate_b, W1, b1, W2, b2):
        import jax, jax.numpy as jnp
        import numpy as np
        B, T, D, H, E = (16, 512, 256, 512, 8)
        Bb, Tt, Dd = x.shape
        Ee = gate_w.shape[1]
        xf = x.reshape(-1, Dd)
        N = xf.shape[0]
        logits = xf @ gate_w + gate_b
        probs = jax.nn.softmax(logits, axis=-1)
        top2_vals, top2_idx = jax.lax.top_k(probs, 2)
        cw = jnp.zeros((N, Ee), dtype=xf.dtype).at[jnp.arange(N)[:, None], top2_idx].add(top2_vals)

        def step(acc, params):
            w1, bb1, w2, bb2, we = params
            h = jax.nn.gelu(xf @ w1 + bb1, approximate=False)
            y = h @ w2 + bb2
            return (acc + we[:, None] * y, None)
        out, _ = jax.lax.scan(step, jnp.zeros_like(xf), (W1, b1, W2, b2, cw.T))
        return out.reshape(Bb, Tt, Dd)
    edge_index = jnp.stack([src, dst])
    x = x + _L0_gnn_ref(_layernorm(x, axis=-1), edge_index, L0_gnn_weight, L0_gnn_attn_l, L0_gnn_attn_r)
    x = x + _L0_ffn_ref(_layernorm(x, axis=-1)[None], L0_ffn_gate_w, L0_ffn_gate_b, L0_ffn_W1, L0_ffn_b1, L0_ffn_W2, L0_ffn_b2)[0]
    return x

_drawn_inputs = setup_inputs


def setup_inputs(seed=0):
    import zlib

    import numpy as np

    out = dict(_drawn_inputs(seed))
    spreads = {'L0_ffn_gate_b': (0.0, 0.509), 'L0_ffn_b1': (0.0, 0.8), 'L0_ffn_b2': (0.0, 0.373)}
    factors = {'L0_ffn_W1': 3.412, 'L0_ffn_W2': 3.2}
    for name, (base, spread) in spreads.items():
        noise = np.random.default_rng([zlib.crc32(name.encode()), seed]).standard_normal(out[name].shape)
        drawn = base * np.exp(spread * noise) if base else spread * noise
        out[name] = jnp.asarray(drawn.astype(out[name].dtype))
    for name, factor in factors.items():
        out[name] = (out[name] * factor).astype(out[name].dtype)
    return out
```

```python
from contextlib import ExitStack

import concourse.bass as bass
from concourse import mybir

F32 = mybir.dt.float32
F32R = mybir.dt.float32r
BF16 = mybir.dt.bfloat16
I32 = mybir.dt.int32
U32 = mybir.dt.uint32
ALU = mybir.AluOpType
ACT = mybir.ActivationFunctionType
AX = mybir.AxisListType
ds = bass.ds

P = 128
TOP = 2
GT = 7
EPS = 1e-5
SLOPE = 0.01
N_STEPS = 43
N_FOLD = 4
FAR = 1.0e6


def padded_nodes(n):
    return -(-n // (P * GT)) * P * GT


def pieces(n, experts):
    most = (TOP * n + experts * (P - 1)) // P
    least = -(-TOP * n // P)
    tiles = most + most % 2
    return tiles, tiles - least


class Steps:

    def __init__(self, engine, sem, per_group=0):
        self.engine, self.sem, self.per = engine, sem, per_group
        self.base, self.n = 0, 0

    def begin(self, g):
        self.base, self.n = g * self.per, 0

    def end(self):
        assert self.n == self.per, (self.n, self.per)

    def did(self, ins):
        ins.then_inc(self.sem, 1)
        self.n += 1

    def wait(self):
        self.engine.wait_ge(self.sem, self.base + self.n)


def gnn_moe(nc, n, x, edges, gw, attn_l, attn_r, gate_w, gate_b, w1, b1, w2, b2, out):
    D = x.shape[1]
    H, DH = attn_l.shape
    E = gate_w.shape[1]
    HID = w1.shape[2]
    KC = D // P
    HC = HID // P
    NP = padded_nodes(n)
    GROUPS = NP // (P * GT)
    TILES, DUMMIES = pieces(n, E)
    ROW = D + 1 + E
    TOK, CW = D, D + 1
    CAP = NP + P
    XS_ROWS = E * CAP + DUMMIES * P
    assert E == GROUPS + 1
    ZEROS = 16 * (-(-DUMMIES // GT) - (-(1 + DUMMIES) // GT))
    assert out.shape[0] == NP + P * (1 + DUMMIES)

    xs = nc.dram_tensor("dispatched_rows", [XS_ROWS, ROW], F32).ap()

    with ExitStack() as ctx:
        def sb(name, shape, dt=F32):
            return ctx.enter_context(nc.sbuf_tensor(name, shape, dt))

        def sem(name):
            return ctx.enter_context(nc.semaphore(name))

        bank = [ctx.enter_context(nc.psum_tensor(f"bank{i}", [P, 512], F32)) for i in range(8)]

        turn_d, turn_s = (bank[0], bank[5]), (bank[1], bank[7])

        w1hi = sb("w1hi", [P, E * KC * HID], F32R)
        w1lo = sb("w1lo", [P, E * KC * HID], F32R)
        w2hi = sb("w2hi", [P, E * HC * D], F32R)
        w2lo = sb("w2lo", [P, E * HC * D], F32R)
        w1s = sb("w1_stage", [P, KC * HID])
        w2s = sb("w2_stage", [P, HC * D])
        b2sb = sb("b2sb", [E, D])
        ident = sb("ident", [P, P])
        upper = sb("upper", [P, P], BF16)
        ones = sb("ones", [P, P], BF16)
        tokid = sb("tokid", [P, NP // P], I32)
        far = sb("far", [P, NP // P])
        keep = sb("keep", [P, NP // P])
        iota_e = sb("iota_e", [P, E])
        region0 = sb("region0", [P, E])
        one8 = sb("one8", [P, E])
        iota_j = sb("iota_j", [1, TILES])
        padrow = sb("padrow", [P, ROW])
        wcat = sb("wcat", [P, KC, D + 2 * H])
        gatew = sb("gatew", [P, KC, E])
        gateb = sb("gateb", [P, E])
        edge = sb("edge", [P, GROUPS, 2 * GT], I32)
        edge_g = sb("edge_g", [P, 2 * GT], I32)
        shared = sb("shared", [P, 4 * GT * D])

        def part(k):
            return shared[:, k * GT * D:(k + 1) * GT * D].rearrange("p (t d) -> p t d", t=GT)

        gd, gs, xg, xdT = part(0), part(1), part(2), part(3)
        rows = sb("rows", [P, GT, ROW])
        turned = sb("turned", [P, 4 * D])
        xsT = turned[:, 0:2 * D].rearrange("p (t d) -> p t d", t=2)
        x2T = turned[:, 2 * D:4 * D].rearrange("p (t d) -> p t d", t=2)
        cwT = turned[0:E, 0:GT * P]
        attnl, attnr = turned[:, 0:D], turned[:, D:2 * D]
        st = sb("st", [P, 2 * GT, 6])
        ln = {1: [sb(f"ln1_{i}", [P, 2 * GT]) for i in range(10)], 2: [sb(f"ln2_{i}", [P, GT]) for i in range(10)]}
        sc = sb("sc", [P, GT, H])
        lr = sb("lr", [P, GT, H])
        hm = sb("hm", [P, GT])
        he = sb("he", [P, GT, H])
        hsum = sb("hsum", [P, GT])
        hrec = sb("hrec", [P, GT])
        alpha = sb("alpha", [P, GT, H])
        prod = sb("prod", [P, 2, D])
        msg = sb("msg", [P, 2, DH])
        lg = sb("lg", [P, GT, E])
        mx = sb("mx", [P, GT, 8])
        mi = sb("mi", [P, GT, 8], U32)
        mif = sb("mif", [P, GT, TOP])
        em = sb("em", [P, GT, E])
        ex = sb("ex", [P, GT, E])
        esum = sb("esum", [P, GT])
        erec = sb("erec", [P, GT])
        pr = sb("pr", [P, GT, E])
        pm = sb("pm", [P, GT, E])
        mask = sb("mask", [P, GT, TOP, E])
        both = sb("both", [P, GT, E])
        both16 = sb("both16", [P, GT, E], BF16)
        rank = sb("rank", [P, GT, E])
        mrank = sb("mrank", [P, GT, TOP, E])
        posf = sb("posf", [P, GT, TOP])
        posi = sb("posi", [P, GT, TOP], I32)
        filled = sb("filled", [P, E])
        filled_i = sb("filled_i", [1, E], I32)
        cnt = sb("cnt", [1, E])
        cnt_i = sb("cnt_i", [1, E], I32)
        nt_i = sb("nt_i", [1, E], I32)
        nt = sb("nt", [1, E])
        upto = sb("upto", [1, E])
        TE = TILES * E
        ge = shared[0:1, 3 * GT * D:3 * GT * D + TE].rearrange("p (j e) -> p j e", e=E)
        gn = w1s[0:1, 0:TE].rearrange("p (j e) -> p j e", e=E)
        tf = sb("tf", [1, 4, TILES])
        ti = sb("ti", [1, 6, TILES], I32)
        BASE = E * HID
        b1bc = shared[:, 0:BASE]
        hb = shared[:, BASE:BASE + 2 * HID].rearrange("p (s m) -> p s m", s=2)
        yb = shared[:, BASE + 2 * HID:BASE + 2 * HID + 2 * D].rearrange("p (s m) -> p s m", s=2)
        BASE += 2 * HID + 2 * D
        xin = shared[:, BASE:BASE + 2 * ROW].rearrange("p (s m) -> p s m", s=2)
        assert BASE + 2 * ROW <= 4 * GT * D
        xThi = sb("xThi", [P, 2, KC * P], F32R)
        xTlo = sb("xTlo", [P, 2, KC * P], F32R)
        hThi = sb("hThi", [P, 2, HID], F32R)
        hTlo = sb("hTlo", [P, 2, HID], F32R)
        tokring = sb("tokring", [P, TILES], I32)
        cwring = sb("cwring", [P, TILES])
        toknow = sb("toknow", [P, 2], I32)

        s_edge, s_const, s_vw, s_bias = sem("s_edge"), sem("s_const"), sem("s_vw"), sem("s_bias")
        s_w, s_whi, s_wlo = sem("s_w"), sem("s_whi"), sem("s_wlo")
        s_pool, s_zero, s_fold = sem("s_pool"), sem("s_zero"), sem("s_fold")
        s_gath = [sem(f"s_gath{i}") for i in range(GT)]
        s_scat = [sem(f"s_scat{i}") for i in range(GT)]
        s_edge_g = sem("s_edge_g")
        s_steps = sem("s_steps")
        s_settled = sem("s_settled")
        s_lnv, s_b1 = sem("s_lnv"), sem("s_b1")
        s_veps, s_y0, s_rstd = sem("s_veps"), sem("s_y0"), sem("s_rstd")
        s_nd, s_ns, s_td, s_ts, s_ed, s_es = (sem(k) for k in ("s_nd", "s_ns", "s_td", "s_ts", "s_ed", "s_es"))
        s_scores, s_harg, s_hexp = sem("s_scores"), sem("s_harg"), sem("s_hexp")
        s_xt, s_prod = sem("s_xt"), sem("s_prod")
        s_nr, s_t2, s_e2, s_gate = sem("s_nr"), sem("s_t2"), sem("s_e2"), sem("s_gate")
        s_garg, s_gexp, s_both, s_ranks = sem("s_garg"), sem("s_gexp"), sem("s_both"), sem("s_ranks")
        s_pos, s_cw, s_cwt, s_ecw = sem("s_pos"), sem("s_cw"), sem("s_cwt"), sem("s_ecw")
        s_b2, s_x2f = sem("s_b2"), sem("s_x2f")
        s_xin, s_out = sem("s_xin"), sem("s_out")
        s_tab, s_tables, s_pads = sem("s_tab"), sem("s_tables"), sem("s_pads")
        p_xin = [sem(f"p_xin{i}") for i in range(2)]
        p_add = [sem(f"p_add{i}") for i in range(2)]
        p_xT, p_xhi, p_xlo, p_h, p_bias, p_gelu, p_hT, p_hhi, p_hlo, p_y, p_yout, p_meta, p_tok = (
            sem(k) for k in ("p_xT", "p_xhi", "p_xlo", "p_h", "p_bias", "p_gelu", "p_hT", "p_hhi", "p_hlo", "p_y",
                             "p_yout", "p_meta", "p_tok"))

        block = ctx.enter_context(nc.Block())
        LAST = GROUPS - 1

        def tile_rows(dram, g):
            r = g * (GT * P)
            part = dram[r:r + GT * P, :] if isinstance(g, int) else dram[ds(r, GT * P), :]
            return part.rearrange("(t p) c -> p t c", p=P)

        @block.sync
        def _(sp):
            sp.dma_start(edge[:, :, :], edges).then_inc(s_edge, 16)

            def load_x(g):
                sp.dma_start(xg[:, :, :], tile_rows(x, g)).then_inc(s_xin, 16)

            def load_expert(e):
                a = w1[e:e + 1] if isinstance(e, int) else w1[ds(e, 1)]
                b = w2[e:e + 1] if isinstance(e, int) else w2[ds(e, 1)]
                sp.dma_start(w1s[:, :].rearrange("p (c m) -> p c m", c=KC),
                             a.rearrange("e (c p) m -> p (e c) m", p=P)).then_inc(s_w, 16)
                sp.dma_start(w2s[:, :].rearrange("p (c m) -> p c m", c=HC),
                             b.rearrange("e (c p) m -> p (e c) m", p=P)).then_inc(s_w, 16)

            sp.dma_start(wcat[:, :, 0:D], gw.rearrange("(c p) m -> p c m", p=P)).then_inc(s_vw, 16)
            sp.dma_start(attnl[:, :], attn_l.rearrange("h d -> (h d)").partition_broadcast(P)).then_inc(s_vw, 16)
            sp.dma_start(attnr[:, :], attn_r.rearrange("h d -> (h d)").partition_broadcast(P)).then_inc(s_vw, 16)
            load_expert(0)
            load_x(0)
            sp.dma_start(gatew[:, :, :], gate_w.rearrange("(c p) m -> p c m", p=P)).then_inc(s_bias, 16)
            sp.dma_start(gateb[:, :], gate_b.partition_broadcast(P)).then_inc(s_bias, 16)
            sp.dma_start(b2sb[:, :], b2).then_inc(s_bias, 16)

            def group(g, last):
                sp.wait_ge(s_wlo, 2 * (g + 1))
                load_expert(g + 1)
                sp.wait_ge(s_x2f, GT * (g + 1))
                sp.dma_start(tile_rows(out, g), xg[:, :, :]).then_inc(s_out, 16)
                if not last:
                    sp.wait_ge(s_out, 16 * (g + 1))
                    load_x(g + 1)

            with sp.Fori(0, LAST) as g:
                group(g, False)
            group(LAST, True)

            sp.wait_ge(s_out, 16 * GROUPS)
            sp.wait_ge(s_tables, 1)
            sp.dma_start(b1bc, b1.rearrange("e m -> (e m)").partition_broadcast(P)).then_inc(s_b1, 16)
            sp.wait_ge(s_pool, 1)
            for e in range(E):
                r = sp.value_load(filled_i[0:1, e:e + 1], min_val=e * CAP, max_val=e * CAP + NP)
                sp.dma_start(xs[ds(r, P), :], padrow[:, :]).then_inc(s_pads, 16)
            sp.wait_ge(s_pads, 16 * E)
            sp.wait_ge(s_zero, ZEROS)
            for i in range(GT):
                sp.wait_ge(s_scat[i], 32 * GROUPS)

            def load_tile(j, s, fresh):
                if not fresh:
                    sp.wait_ge(p_xT, j - 1)
                    sp.wait_ge(p_meta, j - 1)
                r = sp.value_load(ti[0:1, 1, ds(j, 1)], min_val=0, max_val=XS_ROWS - P)
                sp.dma_start(xin[:, s, :], xs[ds(r, P), :]).then_inc(p_xin[s], 16)

            load_tile(0, 0, True)
            load_tile(1, 1, True)
            with sp.Fori(1, TILES // 2) as k:
                load_tile(2 * k, 0, False)
                load_tile(2 * k + 1, 1, False)

        @block.gpsimd
        def _(pool):
            pool.memset(rows[:, :, :], 0.0).then_inc(s_const, 1)
            pool.memset(padrow[:, :], 0.0).then_inc(s_const, 1)
            pool.memset(ident[:, :], 0.0).then_inc(s_const, 1)
            pool.memset(upper[:, :], 1.0).then_inc(s_const, 1)
            pool.memset(ones[:, :], 1.0).then_inc(s_const, 1)
            pool.memset(one8[:, :], 1.0).then_inc(s_const, 1)
            pool.iota(tokid[:, :], [[P, NP // P]], base=0, channel_multiplier=1).then_inc(s_const, 1)
            pool.memset(keep[:, :], 1.0).then_inc(s_const, 1)
            pool.memset(far[:, :], 0.0).then_inc(s_const, 1)
            pool.iota(iota_e[:, :], [[1, E]], base=0, channel_multiplier=0,
                      allow_small_or_imprecise_dtypes=True).then_inc(s_const, 1)
            pool.iota(region0[:, :], [[CAP, E]], base=0, channel_multiplier=0,
                      allow_small_or_imprecise_dtypes=True).then_inc(s_const, 1)
            pool.iota(filled[:, :], [[CAP, E]], base=0, channel_multiplier=0,
                      allow_small_or_imprecise_dtypes=True).then_inc(s_const, 1)
            pool.iota(iota_j[:, :], [[1, TILES]], base=0, channel_multiplier=0,
                      allow_small_or_imprecise_dtypes=True).then_inc(s_const, 1)
            pool.wait_ge(s_const, 13)
            pool.affine_select(ident[:, :], ident[:, :], [[1, P]], ALU.not_equal, 1.0, base=0,
                               channel_multiplier=-1).then_inc(s_const, 1)
            pool.affine_select(upper[:, :], upper[:, :], [[1, P]], ALU.is_gt, 0.0, base=0,
                               channel_multiplier=-1).then_inc(s_const, 1)
            pool.affine_select(keep[:, :], keep[:, :], [[-P, NP // P]], ALU.is_gt, 0.0, base=n,
                               channel_multiplier=-1).then_inc(s_const, 1)
            pool.affine_select(far[:, :], far[:, :], [[-P, NP // P]], ALU.is_gt, FAR, base=n,
                               channel_multiplier=-1).then_inc(s_const, 1)
            pool.iota(rows[:, :, TOK:TOK + 1].bitcast(I32), [[P, GT], [1, 1]], base=NP,
                      channel_multiplier=1).then_inc(s_const, 1)
            pool.iota(padrow[:, TOK:TOK + 1].bitcast(I32), [[1, 1]], base=NP, channel_multiplier=1).then_inc(s_pool, 1)
            pool.wait_ge(s_edge, 16)

            def settle():
                pool.sem_inc(s_settled, 1)

            def gathers(g, first):
                if not first:
                    for i in range(GT):
                        pool.wait_ge(s_gath[i], 32 * g)
                at = edge[:, g, :] if isinstance(g, int) else edge[:, ds(g, 1), :].rearrange("p a t -> p (a t)")
                pool.tensor_copy(edge_g[:, :], at).then_inc(s_edge_g, 1)
                pool.wait_ge(s_edge_g, g + 1)
                for i in range(GT):
                    if not first:
                        pool.wait_ge(s_td, GT * (g - 1) + i + 1)
                        pool.wait_ge(s_ts, GT * (g - 1) + i + 1)
                    settle()
                    pool.indirect_dma_start(gd[:, i, :], None, x,
                                            bass.IndirectOffsetOnAxis(edge_g[:, i:i + 1], 0)).then_inc(s_gath[i], 16)
                    pool.indirect_dma_start(gs[:, i, :], None, x,
                                            bass.IndirectOffsetOnAxis(edge_g[:, GT + i:GT + i + 1], 0)
                                            ).then_inc(s_gath[i], 16)

            def scatters(g):
                pool.wait_ge(s_pos, g + 1)
                settle()
                for i in range(GT):
                    for k in range(TOP):
                        pool.indirect_dma_start(xs, bass.IndirectOffsetOnAxis(posi[:, i, k:k + 1], 0), rows[:, i, :],
                                                None, bounds_check=XS_ROWS - 1, oob_is_err=False
                                                ).then_inc(s_scat[i], 16)

            gathers(0, True)
            pool.wait_ge(s_const, 18)
            for t0 in range(0, DUMMIES, GT):
                m = min(GT, DUMMIES - t0)
                pool.dma_start(xs[E * CAP + t0 * P:E * CAP + (t0 + m) * P, :].rearrange("(t p) c -> p t c", p=P),
                               rows[:, 0:m, :]).then_inc(s_zero, 16)
            for t0 in range(0, 1 + DUMMIES, GT):
                m = min(GT, 1 + DUMMIES - t0)
                pool.dma_start(out[NP + t0 * P:NP + (t0 + m) * P, :].rearrange("(t p) c -> p t c", p=P),
                               rows[:, 0:m, 0:D]).then_inc(s_zero, 16)
            gathers(1, False)
            scatters(0)
            with pool.Fori(1, LAST) as g:
                gathers(g + 1, False)
                scatters(g)
            scatters(LAST)

            pool.wait_ge(s_tables, 1)
            pool.wait_ge(s_out, 16 * GROUPS)
            pool.wait_ge(s_zero, ZEROS)

            def keep_meta(j, s):
                pool.wait_ge(p_xin[s], 16 * (half(j) + 1))
                settle()
                e = pool.value_load(ti[0:1, 0, ds(j, 1)], min_val=0, max_val=E - 1)
                pool.tensor_copy(cwring[:, ds(j, 1)], xin[:, s, ds(e + CW, 1)])
                pool.tensor_copy(tokring[:, ds(j, 1)], xin[:, s, TOK:TOK + 1].bitcast(I32)).then_inc(p_meta, 1)

            def half(j):
                return j // 2 if isinstance(j, int) else j >> 1

            def add_tile(j, s):
                first = isinstance(j, int) and j < 2
                if not first:
                    pool.wait_ge(p_add[s], 16 * half(j))
                pool.wait_ge(p_meta, j + 1)
                pool.tensor_copy(toknow[:, s:s + 1], tokring[:, ds(j, 1)]).then_inc(p_tok, 1)
                pool.wait_ge(p_tok, j + 1)
                for q in range(2):
                    if not first or (q == 0 and j == 1):
                        settle()
                        before = pool.value_load(ti[0:1, 2 + q, ds(j, 1)], min_val=16, max_val=16 * TILES)
                        pool.wait_ge(p_add[q], before)
                pool.wait_ge(p_yout, j + 1)
                settle()
                pool.indirect_dma_start(out, bass.IndirectOffsetOnAxis(toknow[:, s:s + 1], 0), yb[:, s, :], None,
                                        compute_op=ALU.add).then_inc(p_add[s], 16)

            keep_meta(0, 0)
            keep_meta(1, 1)
            for s in range(2):
                keep_meta(2 + s, s)
                add_tile(s, s)
            with pool.Fori(1, TILES // 2 - 1) as k:
                for s in range(2):
                    keep_meta(2 * k + 2 + s, s)
                    add_tile(2 * k + s, s)
            for s in range(2):
                add_tile(TILES - 2 + s, s)
            for s in range(2):
                pool.wait_ge(p_add[s], 16 * (TILES // 2))

        @block.scalar
        def _(act):
            def split_high(e):
                act.wait_ge(s_w, 32 * (e + 1))
                act.activation(w1hi[:, ds(e * (KC * HID), KC * HID)], w1s[:, :], ACT.Copy).then_inc(s_whi, 1)
                act.activation(w2hi[:, ds(e * (HC * D), HC * D)], w2s[:, :], ACT.Copy).then_inc(s_whi, 1)

            def rsqrt_start(g, which):
                v, y = ln[which][5], ln[which][6]
                act.wait_ge(s_veps, 2 * g + which)
                act.activation(ln[which][9][:, :], v[:, :], ACT.Ln).then_inc(s_lnv, 1)
                act.wait_ge(s_lnv, 2 * g + which)
                act.activation(y[:, :], ln[which][9][:, :], ACT.Exp, scale=-0.5).then_inc(s_y0, 1)

            split_high(0)

            def group(g):
                split_high(g + 1)
                rsqrt_start(g, 1)
                act.wait_ge(s_rstd, 2 * g + 1)

                def evacuate(i):
                    act.wait_ge(s_td, GT * g + i + 1)
                    act.activation(xdT[:, i, :], turn_d[i % 2][:, 0:D],
                                   ACT.Copy).then_inc(s_ed, 1)
                    act.wait_ge(s_ts, GT * g + i + 1)
                    act.activation(xsT[:, i % 2, :], turn_s[i % 2][:, 0:D],
                                   ACT.Copy).then_inc(s_es, 1)

                for i in range(GT):
                    act.activation(gs[:, i, :], gs[:, i, :], ACT.Identity, bias=ln[1][8][:, GT + i:GT + i + 1],
                                   scale=ln[1][7][:, GT + i:GT + i + 1]).then_inc(s_ns, 1)
                    if i:
                        evacuate(i - 1)
                evacuate(GT - 1)
                act.wait_ge(s_harg, g + 1)
                act.activation(he[:, :, :], he[:, :, :], ACT.Exp).then_inc(s_hexp, 1)
                rsqrt_start(g, 2)
                for i in range(GT):
                    act.wait_ge(s_t2, GT * g + i + 1)
                    act.activation(x2T[:, i % 2, :], turn_d[i % 2][:, 0:D],
                                   ACT.Copy).then_inc(s_e2, 1)
                act.wait_ge(s_garg, g + 1)
                act.activation(ex[:, :, :], em[:, :, :], ACT.Exp).then_inc(s_gexp, 1)
                act.wait_ge(s_cwt, 2 * g + 1)
                act.activation(cwT[:, 0:4 * P], bank[7][0:E, :], ACT.Copy).then_inc(s_ecw, 1)
                act.wait_ge(s_cwt, 2 * g + 2)
                act.activation(cwT[:, 4 * P:GT * P], bank[1][0:E, 0:(GT - 4) * P], ACT.Copy).then_inc(s_ecw, 1)

            with act.Fori(0, GROUPS) as g:
                group(g)

            def half(j):
                return j // 2 if isinstance(j, int) else j >> 1

            def x_high(j, s):
                act.wait_ge(p_xT, j + 1)
                if not isinstance(j, int) or j >= 2:
                    act.wait_ge(p_h, j - 1)
                act.activation(xThi[:, s, :], bank[0][:, 0:D], ACT.Copy).then_inc(p_xhi, 1)

            def gelu(j, s):
                act.wait_ge(p_bias, j + 1)
                act.activation(hb[:, s, :], hb[:, s, :], ACT.Gelu).then_inc(p_gelu, 1)

            def h_high(j, s):
                act.wait_ge(p_hT, j + 1)
                if not isinstance(j, int) or j >= 2:
                    act.wait_ge(p_y, j - 1)
                act.activation(hThi[:, s, :], bank[3 + s][:, :], ACT.Copy).then_inc(p_hhi, 1)

            def y_out(j, s):
                act.wait_ge(p_y, j + 1)
                act.wait_ge(p_meta, j + 1)
                if not isinstance(j, int) or j >= 2:
                    act.wait_ge(p_add[s], 16 * half(j))
                act.activation(yb[:, s, :], bank[5 + s][:, 0:D], ACT.Copy, scale=cwring[:, ds(j, 1)]).then_inc(p_yout, 1)

            x_high(0, 0)
            gelu(0, 0)
            x_high(1, 1)
            gelu(1, 1)
            x_high(2, 0)
            h_high(0, 0)

            def step(j, s):
                gelu(j, s)
                y_out(j - 2, s)
                if not (isinstance(j, int) and j + 1 >= TILES):
                    x_high(j + 1, 1 - s)
                h_high(j - 1, 1 - s)

            step(2, 0)
            step(3, 1)
            with act.Fori(2, TILES // 2 - 1) as k:
                step(2 * k, 0)
                step(2 * k + 1, 1)
            step(TILES - 2, 0)
            step(TILES - 1, 1)
            y_out(TILES - 2, 0)
            h_high(TILES - 1, 1)
            y_out(TILES - 1, 1)

        @block.vector
        def _(dve):
            def split_low(e):
                a, b = e * (KC * HID), e * (HC * D)
                dve.wait_ge(s_whi, 2 * e + 1)
                dve.tensor_tensor(w1lo[:, ds(a, KC * HID)], w1s[:, :], w1hi[:, ds(a, KC * HID)].bitcast(F32),
                                  ALU.subtract).then_inc(s_wlo, 1)
                dve.wait_ge(s_whi, 2 * e + 2)
                dve.tensor_tensor(w2lo[:, ds(b, HC * D)], w2s[:, :], w2hi[:, ds(b, HC * D)].bitcast(F32),
                                  ALU.subtract).then_inc(s_wlo, 1)

            dve.wait_ge(s_vw, 48)
            fold = Steps(dve, s_fold)
            for a, at in ((attnr, D), (attnl, D + H)):
                fold.did(dve.tensor_tensor(prod[:, :, :], wcat[:, :, 0:D],
                                           a[:, :].unsqueeze(1).to_broadcast([P, KC, D]), ALU.mult))
                fold.wait()
                fold.did(dve.tensor_reduce(wcat[:, :, at:at + H],
                                           prod[:, :, :].rearrange("p c (h d) -> p c h d", h=H), AX.X, ALU.add))
                fold.wait()
            FOLDS = fold.n
            assert FOLDS == N_FOLD
            split_low(0)
            dve.wait_ge(s_const, 18)

            t = Steps(dve, s_steps, N_STEPS)

            def variance(g, which):
                m = 2 * GT if which == 1 else GT
                msum, md, vs, md2, vs2, veps = (b[:, :] for b in ln[which][0:6])
                s3 = st[:, 0:m, :]
                dve.tensor_tensor(msum, s3[:, :, 1], s3[:, :, 4], ALU.add)
                dve.tensor_tensor(vs, s3[:, :, 2], s3[:, :, 5], ALU.add)
                t.did(dve.tensor_tensor(md, s3[:, :, 1], s3[:, :, 4], ALU.subtract))
                t.wait()
                dve.tensor_tensor(md2, md, md, ALU.mult)
                t.did(dve.tensor_scalar(vs2, vs, 1.0 / D, EPS, ALU.mult, ALU.add))
                t.wait()
                dve.scalar_tensor_tensor(veps, md2, 0.25, vs2, ALU.mult, ALU.add).then_inc(s_veps, 1)

            def rstd(g, which):
                msum, t1, t2, mean, veps, y, r, nmr = (ln[which][k][:, :] for k in (0, 1, 2, 3, 5, 6, 7, 8))
                dve.wait_ge(s_y0, 2 * g + which)
                t.did(dve.tensor_tensor(t1, y, veps, ALU.mult))
                t.wait()
                dve.tensor_scalar(mean, msum, 0.5, None, ALU.mult)
                t.did(dve.scalar_tensor_tensor(t2, t1, -0.5, y, ALU.mult, ALU.mult))
                t.wait()
                t.did(dve.scalar_tensor_tensor(r, t2, 1.5, y, ALU.add, ALU.mult))
                t.wait()
                dve.scalar_tensor_tensor(nmr, mean, -1.0, r, ALU.mult, ALU.mult).then_inc(s_rstd, 1)
                dve.wait_ge(s_rstd, 2 * g + which)

            def group(g):
                first = isinstance(g, int) and g == 0
                split_low(g + 1)
                for i in range(GT):
                    dve.wait_ge(s_gath[i], 32 * (g + 1))
                    dve.bn_stats(st[:, i, :], gd[:, i, :])
                    ins = dve.bn_stats(st[:, GT + i, :], gs[:, i, :])
                t.begin(g)
                t.did(ins)
                t.wait()
                variance(g, 1)
                rstd(g, 1)
                for i in range(GT):
                    dve.tensor_scalar(gd[:, i, :], gd[:, i, :], ln[1][3][:, i:i + 1], ln[1][7][:, i:i + 1],
                                      ALU.subtract, ALU.mult).then_inc(s_nd, 1)
                dve.wait_ge(s_scores, g + 1)
                t.did(dve.tensor_copy(sc[:, :, :], bank[2][:, 0:GT * H].rearrange("p (t h) -> p t h", h=H)))
                t.wait()
                t.did(dve.scalar_tensor_tensor(lr[:, :, :], sc[:, :, :], SLOPE, sc[:, :, :], ALU.mult, ALU.max))
                t.wait()
                t.did(dve.tensor_reduce(hm[:, :], lr[:, :, :], AX.X, ALU.max))
                t.wait()
                dve.tensor_tensor(he[:, :, :], lr[:, :, :], hm[:, :].unsqueeze(2).to_broadcast([P, GT, H]),
                                  ALU.subtract).then_inc(s_harg, 1)
                dve.wait_ge(s_hexp, g + 1)
                t.did(dve.tensor_reduce(hsum[:, :], he[:, :, :], AX.X, ALU.add))
                t.wait()
                t.did(dve.reciprocal(hrec[:, :], hsum[:, :]))
                t.wait()
                t.did(dve.tensor_tensor(alpha[:, :, :], he[:, :, :], hrec[:, :].unsqueeze(2).to_broadcast([P, GT, H]),
                                        ALU.mult))
                t.wait()
                dve.wait_ge(s_xin, 16 * (g + 1))
                for i in range(GT):
                    dve.wait_ge(s_xt, GT * g + i + 1)
                    dve.tensor_tensor(prod[:, i % 2, :].rearrange("p (h d) -> p h d", h=H),
                                      bank[3 + i % 2][:, 0:D].rearrange("p (h d) -> p h d", h=H),
                                      alpha[:, i, :].unsqueeze(2).to_broadcast([P, H, DH]), ALU.mult
                                      ).then_inc(s_prod, 1)
                    dve.wait_ge(s_prod, GT * g + i + 1)
                    t.did(dve.tensor_reduce(msg[:, i % 2, :], prod[:, i % 2, :].rearrange("p (h d) -> p d h", h=H),
                                            AX.X, ALU.add))
                    t.wait()
                    xv = xg[:, i, :].rearrange("p (h d) -> p h d", h=H)
                    t.did(dve.tensor_tensor(xv, xv, msg[:, i % 2, :].unsqueeze(1).to_broadcast([P, H, DH]), ALU.add))
                    t.wait()
                    ins = dve.bn_stats(st[:, i, :], xg[:, i, :])
                t.did(ins)
                t.wait()
                variance(g, 2)
                rstd(g, 2)
                if first:
                    dve.wait_ge(s_zero, ZEROS)
                for i in range(GT):
                    if not first:
                        dve.wait_ge(s_scat[i], 32 * g)
                    dve.tensor_scalar(rows[:, i, 0:D], xg[:, i, :], ln[2][3][:, i:i + 1], ln[2][7][:, i:i + 1],
                                      ALU.subtract, ALU.mult).then_inc(s_nr, 1)
                at = ds(g * GT, GT)
                dve.wait_ge(s_gate, g + 1)
                t.did(dve.tensor_tensor(lg[:, :, :], bank[2][:, 64:64 + GT * E].rearrange("p (t e) -> p t e", e=E),
                                        gateb[:, :].unsqueeze(1).to_broadcast([P, GT, E]), ALU.add))
                t.wait()
                dve.tensor_copy(rows[:, 0:GT, TOK].bitcast(I32), tokid[:, at])
                for i in range(GT):
                    ins = dve.max(mx[:, i, :], lg[:, i, :])
                t.did(ins)
                t.wait()
                dve.tensor_tensor(em[:, :, :], lg[:, :, :], mx[:, :, 0:1].to_broadcast([P, GT, E]),
                                  ALU.subtract).then_inc(s_garg, 1)
                for i in range(GT):
                    ins = dve.max_index(mi[:, i, :], mx[:, i, :], lg[:, i, :])
                t.did(ins)
                t.wait()
                t.did(dve.tensor_copy(mif[:, :, :], mi[:, :, 0:TOP]))
                t.wait()
                t.did(dve.tensor_tensor(mask[:, :, :, :], mif[:, :, :].unsqueeze(3).to_broadcast([P, GT, TOP, E]),
                                        iota_e[:, :].unsqueeze(1).unsqueeze(1).to_broadcast([P, GT, TOP, E]),
                                        ALU.is_equal))
                t.wait()
                t.did(dve.tensor_tensor(both[:, :, :], mask[:, :, 0, :], mask[:, :, 1, :], ALU.add))
                t.wait()
                dve.tensor_tensor(both16[:, :, :], both[:, :, :], keep[:, at].unsqueeze(2).to_broadcast([P, GT, E]),
                                  ALU.mult).then_inc(s_both, 1)
                dve.wait_ge(s_gexp, g + 1)
                dve.tensor_tensor(pr[:, :, :], ex[:, :, :], both[:, :, :], ALU.mult)
                t.did(dve.tensor_reduce(esum[:, :], ex[:, :, :], AX.X, ALU.add))
                t.wait()
                t.did(dve.reciprocal(erec[:, :], esum[:, :]))
                t.wait()
                dve.tensor_tensor(rows[:, 0:GT, CW:ROW], pr[:, :, :], erec[:, :].unsqueeze(2).to_broadcast([P, GT, E]),
                                  ALU.mult).then_inc(s_cw, 1)
                dve.wait_ge(s_ranks, g + 1)
                t.did(dve.tensor_tensor(rank[:, :, :], bank[6][:, 0:GT * E].rearrange("p (t e) -> p t e", e=E),
                                        filled[:, :].unsqueeze(1).to_broadcast([P, GT, E]), ALU.add))
                t.wait()
                dve.tensor_tensor(filled[:, :], bank[6][:, 64:64 + E], filled[:, :], ALU.add)
                t.did(dve.tensor_tensor(mrank[:, :, :, :], mask[:, :, :, :],
                                        rank[:, :, :].unsqueeze(2).to_broadcast([P, GT, TOP, E]), ALU.mult))
                t.wait()
                t.did(dve.tensor_reduce(posf[:, :, :], mrank[:, :, :, :], AX.X, ALU.add))
                t.wait()
                dve.tensor_tensor(posi[:, :, :], posf[:, :, :], far[:, at].unsqueeze(2).to_broadcast([P, GT, TOP]),
                                  ALU.add).then_inc(s_pos, 1)
                for i in range(GT):
                    dve.wait_ge(s_b2, GT * g + i + 1)
                    dve.tensor_tensor(xg[:, i, :], bank[3 + i % 2][:, 0:D], xg[:, i, :], ALU.add).then_inc(s_x2f, 1)
                t.end()

            group(0)
            with dve.Fori(1, GROUPS) as g:
                group(g)

            u = Steps(dve, s_tab)
            dve.tensor_copy(filled_i[:, :], filled[0:1, :])
            u.did(dve.tensor_tensor(cnt[:, :], filled[0:1, :], region0[0:1, :], ALU.subtract))
            u.wait()
            u.did(dve.tensor_scalar(cnt_i[:, :], cnt[:, :], float(P - 1), None, ALU.add))
            u.wait()
            u.did(dve.tensor_scalar(nt_i[:, :], cnt_i[:, :], P.bit_length() - 1, None, ALU.logical_shift_right))
            u.wait()
            u.did(dve.tensor_copy(nt[:, :], nt_i[:, :]))
            u.wait()
            u.did(dve.tensor_tensor_scan(upto[:, :], one8[0:1, :], nt[:, :], 0.0, ALU.mult, ALU.add))
            u.wait()
            u.did(dve.tensor_tensor(ge[:, :, :], iota_j[:, :].unsqueeze(2).to_broadcast([1, TILES, E]),
                                    upto[:, :].unsqueeze(1).to_broadcast([1, TILES, E]), ALU.is_ge))
            u.wait()
            u.did(dve.tensor_tensor(gn[:, :, :], ge[:, :, :], nt[:, :].unsqueeze(1).to_broadcast([1, TILES, E]),
                                    ALU.mult))
            u.did(dve.tensor_reduce(tf[:, 0, :], ge[:, :, :], AX.X, ALU.add))
            u.wait()
            u.did(dve.tensor_reduce(tf[:, 1, :], gn[:, :, :], AX.X, ALU.add))
            dve.tensor_scalar(ti[:, 0, :], tf[:, 0, :], float(E - 1), None, ALU.min)
            u.wait()
            u.did(dve.tensor_tensor(tf[:, 2, :], iota_j[:, :], tf[:, 1, :], ALU.subtract))
            u.did(dve.tensor_copy(ti[:, 4, :], tf[:, 1, :]))
            u.wait()
            u.did(dve.tensor_scalar(tf[:, 3, :], tf[:, 0, :], float(CAP), None, ALU.mult))
            u.did(dve.tensor_scalar(ti[:, 5, :], tf[:, 1, :], 1.0, None, ALU.add))
            u.wait()
            dve.scalar_tensor_tensor(ti[:, 1, :], tf[:, 2, :], float(P), tf[:, 3, :], ALU.mult, ALU.add)
            u.did(dve.tensor_scalar(ti[:, 4:6, :], ti[:, 4:6, :], 1, None, ALU.logical_shift_right))
            u.wait()
            u.did(dve.tensor_scalar(ti[:, 2, :], ti[:, 5, :], 16.0, 16.0, ALU.mult, ALU.max))
            dve.tensor_scalar(ti[:, 3, :], ti[:, 4, :], 16.0, 16.0, ALU.mult, ALU.max).then_inc(s_tables, 1)

            def add_bias(j, s):
                dve.wait_ge(p_h, j + 1)
                if not isinstance(j, int) or j >= 2:
                    dve.wait_ge(p_hT, j - 1)
                e = dve.value_load(ti[0:1, 0, ds(j, 1)], min_val=0, max_val=E - 1)
                dve.tensor_tensor(hb[:, s, :], bank[1 + s][:, :], b1bc[:, ds(e * HID, HID)],
                                  ALU.add).then_inc(p_bias, 1)

            def x_low(j, s):
                dve.wait_ge(p_xhi, j + 1)
                dve.tensor_tensor(xTlo[:, s, :], bank[0][:, 0:D], xThi[:, s, :].bitcast(F32),
                                  ALU.subtract).then_inc(p_xlo, 1)

            def h_low(j, s):
                dve.wait_ge(p_hhi, j + 1)
                dve.tensor_tensor(hTlo[:, s, :], bank[3 + s][:, :], hThi[:, s, :].bitcast(F32),
                                  ALU.subtract).then_inc(p_hlo, 1)

            dve.wait_ge(s_tables, 1)
            dve.wait_ge(s_b1, 16)
            x_low(0, 0)
            add_bias(0, 0)
            x_low(1, 1)
            add_bias(1, 1)
            x_low(2, 0)
            h_low(0, 0)

            def step(j, s):
                add_bias(j, s)
                if not (isinstance(j, int) and j + 1 >= TILES):
                    x_low(j + 1, 1 - s)
                h_low(j - 1, 1 - s)

            with dve.Fori(1, TILES // 2 - 1) as k:
                step(2 * k, 0)
                step(2 * k + 1, 1)
            step(TILES - 2, 0)
            step(TILES - 1, 1)
            h_low(TILES - 1, 1)

        @block.tensor
        def _(pe):
            pe.wait_ge(s_const, 18)
            pe.wait_ge(s_fold, N_FOLD)
            pe.wait_ge(s_bias, 48)

            def transpose_pair(to, src):
                for c in range(KC):
                    ins = pe.transpose(to[:, c * P:(c + 1) * P], src[:, c * P:(c + 1) * P], ident[:, :])
                return ins

            def scores(g, i):
                pe.wait_ge(s_ed, GT * g + i + 1)
                pe.wait_ge(s_es, GT * g + i + 1)
                o = bank[2][:, i * H:(i + 1) * H]
                for c in range(KC):
                    pe.matmul(o, xdT[:, i, c * P:(c + 1) * P], wcat[:, c, D:D + H], start=c == 0, stop=False)
                for c in range(KC):
                    ins = pe.matmul(o, xsT[:, i % 2, c * P:(c + 1) * P], wcat[:, c, D + H:D + 2 * H], start=False,
                                    stop=c == KC - 1)
                return ins

            def gate(g, i):
                pe.wait_ge(s_e2, GT * g + i + 1)
                for c in range(KC):
                    ins = pe.matmul(bank[2][:, 64 + i * E:64 + (i + 1) * E], x2T[:, i % 2, c * P:(c + 1) * P],
                                    gatew[:, c, :], start=c == 0, stop=c == KC - 1)
                return ins

            def group(g):
                for i in range(GT):
                    pe.wait_ge(s_nd, GT * g + i + 1)
                    transpose_pair(turn_d[i % 2], gd[:, i, :]).then_inc(s_td, 1)
                    pe.wait_ge(s_ns, GT * g + i + 1)
                    transpose_pair(turn_s[i % 2], gs[:, i, :]).then_inc(s_ts, 1)
                    if i:
                        scores(g, i - 1)
                scores(g, GT - 1).then_inc(s_scores, 1)
                for i in range(GT):
                    if i >= 2:
                        pe.wait_ge(s_prod, GT * g + i - 1)
                    for c in range(KC):
                        ins = pe.matmul(bank[3 + i % 2][:, 0:D], xdT[:, i, c * P:(c + 1) * P], wcat[:, c, 0:D],
                                        start=c == 0, stop=c == KC - 1)
                    ins.then_inc(s_xt, 1)
                for i in range(GT):
                    pe.wait_ge(s_nr, GT * g + i + 1)
                    transpose_pair(turn_d[i % 2], rows[:, i, 0:D]).then_inc(s_t2, 1)
                    if i:
                        gate(g, i - 1)
                gate(g, GT - 1).then_inc(s_gate, 1)
                pe.wait_ge(s_both, g + 1)
                r = bank[6][:, 0:GT * E].rearrange("p (t e) -> p t e", e=E)
                pe.matmul(r, upper[:, :], both16[:, :, :], start=True, stop=False)
                for i in range(GT - 1):
                    m = GT - 1 - i
                    pe.matmul(r[:, i + 1:GT, :], ones[:, :], both16[:, i:i + 1, :].to_broadcast([P, m, E]),
                              start=False, stop=i == GT - 2)
                for i in range(GT):
                    ins = pe.matmul(bank[6][:, 64:64 + E], ones[:, :], both16[:, i, :], start=i == 0, stop=i == GT - 1)
                ins.then_inc(s_ranks, 1)
                pe.wait_ge(s_cw, g + 1)
                for i in range(GT):
                    to = bank[7][0:E, i * P:(i + 1) * P] if i < 4 else bank[1][0:E, (i - 4) * P:(i - 3) * P]
                    ins = pe.transpose(to, rows[:, i, CW:ROW], ident[:, :])
                    if i in (3, GT - 1):
                        ins.then_inc(s_cwt, 1)
                for i in range(GT):
                    if i in (0, 4):
                        pe.wait_ge(s_ecw, 2 * g + (1 if i == 0 else 2))
                    if i >= 2:
                        pe.wait_ge(s_x2f, GT * g + i - 1)
                    pe.matmul(bank[3 + i % 2][:, 0:D], cwT[:, i * P:(i + 1) * P], b2sb[:, :], start=True,
                              stop=True).then_inc(s_b2, 1)

            with pe.Fori(0, GROUPS) as g:
                group(g)

            def half(j):
                return j // 2 if isinstance(j, int) else j >> 1

            def turn_x(j, s):
                pe.wait_ge(p_xin[s], 16 * (half(j) + 1))
                if not isinstance(j, int) or j >= 1:
                    pe.wait_ge(p_xlo, j)
                transpose_pair(bank[0], xin[:, s, 0:D]).then_inc(p_xT, 1)

            def first_product(j, s, e):
                pe.wait_ge(p_xhi, j + 1)
                o = bank[1 + s][:, :]
                for c in range(KC):
                    lhs = xThi[:, s, c * P:(c + 1) * P]
                    at = ds(e * (KC * HID) + c * HID, HID)
                    pe.matmul(o, lhs, w1hi[:, at], start=c == 0, stop=False)
                    pe.matmul(o, lhs, w1lo[:, at], start=False, stop=False)
                pe.wait_ge(p_xlo, j + 1)
                for c in range(KC):
                    at = ds(e * (KC * HID) + c * HID, HID)
                    ins = pe.matmul(o, xTlo[:, s, c * P:(c + 1) * P], w1hi[:, at], start=False, stop=c == KC - 1)
                ins.then_inc(p_h, 1)

            def turn_h(j, s):
                pe.wait_ge(p_gelu, j + 1)
                for c in range(HC):
                    ins = pe.transpose(bank[3 + s][:, c * P:(c + 1) * P], hb[:, s, c * P:(c + 1) * P], ident[:, :])
                ins.then_inc(p_hT, 1)

            def second_product(j, s, e):
                pe.wait_ge(p_hhi, j + 1)
                if not isinstance(j, int) or j >= 2:
                    pe.wait_ge(p_yout, j - 1)
                o = bank[5 + s][:, 0:D]
                for c in range(HC):
                    lhs = hThi[:, s, c * P:(c + 1) * P]
                    at = ds(e * (HC * D) + c * D, D)
                    pe.matmul(o, lhs, w2hi[:, at], start=c == 0, stop=False)
                    pe.matmul(o, lhs, w2lo[:, at], start=False, stop=False)
                pe.wait_ge(p_hlo, j + 1)
                for c in range(HC):
                    at = ds(e * (HC * D) + c * D, D)
                    ins = pe.matmul(o, hTlo[:, s, c * P:(c + 1) * P], w2hi[:, at], start=False, stop=c == HC - 1)
                ins.then_inc(p_y, 1)

            def expert(j):
                return pe.value_load(ti[0:1, 0, ds(j, 1)], min_val=0, max_val=E - 1)

            def step(j, s):
                first_product(j, s, expert(j))
                if not isinstance(j, int) or j >= 2:
                    second_product(j - 2, s, expert(j - 2))
                if not (isinstance(j, int) and j + 1 >= TILES):
                    turn_x(j + 1, 1 - s)
                if not isinstance(j, int) or j >= 1:
                    turn_h(j - 1, 1 - s)

            turn_x(0, 0)
            step(0, 0)
            step(1, 1)
            step(2, 0)
            step(3, 1)
            with pe.Fori(2, TILES // 2 - 1) as k:
                step(2 * k, 0)
                step(2 * k + 1, 1)
            step(TILES - 2, 0)
            step(TILES - 1, 1)
            second_product(TILES - 2, 0, expert(TILES - 2))
            turn_h(TILES - 1, 1)
            second_product(TILES - 1, 1, expert(TILES - 1))


def kernel(x, src, dst, L0_gnn_weight, L0_gnn_attn_l, L0_gnn_attn_r, L0_ffn_gate_w, L0_ffn_gate_b, L0_ffn_W1,
           L0_ffn_b1, L0_ffn_W2, L0_ffn_b2):
    import numpy as np
    import concourse.bacc as bacc
    from concourse.bass_utils import run_bass_kernel_spmd

    x = np.asarray(x)
    n = x.shape[0]
    pad = padded_nodes(n) - n
    experts = np.shape(L0_ffn_gate_w)[1]

    def by_tile(index):
        a = np.pad(np.asarray(index)[:n], (0, pad)).reshape(-1, GT, P)
        return a.transpose(2, 0, 1)

    arrays = {
        "x": np.pad(x, ((0, pad), (0, 0))),
        "edges": np.ascontiguousarray(np.concatenate([by_tile(dst), by_tile(src)], axis=2)),
        "gnn_weight": np.ascontiguousarray(L0_gnn_weight),
        "attn_l": np.ascontiguousarray(L0_gnn_attn_l),
        "attn_r": np.ascontiguousarray(L0_gnn_attn_r),
        "gate_w": np.ascontiguousarray(L0_ffn_gate_w),
        "gate_b": np.ascontiguousarray(L0_ffn_gate_b),
        "w1": np.ascontiguousarray(L0_ffn_W1),
        "b1": np.ascontiguousarray(L0_ffn_b1),
        "w2": np.ascontiguousarray(L0_ffn_W2),
        "b2": np.ascontiguousarray(L0_ffn_b2),
    }
    nc = bacc.Bacc("TRN2", target_bir_lowering=False, num_devices=1)
    args = [nc.dram_tensor(k, a.shape, mybir.dt.from_np(a.dtype), kind="ExternalInput").ap()
            for k, a in arrays.items()]
    rows = n + pad + P * (1 + pieces(n, experts)[1])
    out = nc.dram_tensor("out", (rows, x.shape[1]), F32, kind="ExternalOutput").ap()
    gnn_moe(nc, n, *args, out)
    result = run_bass_kernel_spmd(nc, [arrays], core_ids=[0])
    return result.results[0]["out"][:n]
```

```python
from contextlib import ExitStack

import concourse.bass as bass
from concourse import mybir

F32 = mybir.dt.float32
F32R = mybir.dt.float32r
BF16 = mybir.dt.bfloat16
I32 = mybir.dt.int32
U32 = mybir.dt.uint32
ALU = mybir.AluOpType
ACT = mybir.ActivationFunctionType
AX = mybir.AxisListType
ds = bass.ds

P = 128
TOP = 2
GT = 7
EPS = 1e-5
SLOPE = 0.01
A_STEPS = 17
B_STEPS = 33
GUESS = float(0x5F3759DF)
RING = 4
N_FOLD = 4
FAR = 1.0e6


def padded_nodes(n):
    return -(-n // (P * GT)) * P * GT


def pieces(n, experts):
    most = (TOP * n + experts * (P - 1)) // P
    least = -(-TOP * n // P)
    tiles = most + most % 2
    return tiles, tiles - least


def back(i, ring=RING):
    return ring if i >= ring else i + GT - max(k for k in range(GT) if k % ring == i)


class Steps:

    def __init__(self, engine, sem, per_group=0):
        self.engine, self.sem, self.per = engine, sem, per_group
        self.base, self.n = 0, 0

    def begin(self, g):
        self.base, self.n = g * self.per, 0

    def end(self):
        assert self.n == self.per, (self.n, self.per)

    def did(self, ins):
        ins.then_inc(self.sem, 1)
        self.n += 1

    def wait(self):
        self.engine.wait_ge(self.sem, self.base + self.n)


def gnn_moe(nc, n, x, edges, gw, attn_l, attn_r, gate_w, gate_b, w1, b1, w2, b2, out):
    D = x.shape[1]
    H, DH = attn_l.shape
    E = gate_w.shape[1]
    HID = w1.shape[2]
    KC = D // P
    HC = HID // P
    NP = padded_nodes(n)
    GROUPS = NP // (P * GT)
    TILES, DUMMIES = pieces(n, E)
    ROW = D + 1 + E
    TOK, CW = D, D + 1
    CAP = NP + P
    XS_ROWS = E * CAP + DUMMIES * P
    ND = 4
    assert E == GROUPS + 1
    ZEROS = 16 * (-(-DUMMIES // GT) - (-(1 + DUMMIES) // GT))
    assert out.shape[0] == NP + P * (1 + DUMMIES)

    XW = D + H
    xs = nc.dram_tensor("dispatched_rows", [XS_ROWS, ROW], F32).ap()
    table = nc.dram_tensor("transformed_rows", [NP, XW], F32).ap()
    src_scores = nc.dram_tensor("src_scores", [NP, H], F32).ap()

    with ExitStack() as ctx:
        def sb(name, shape, dt=F32):
            return ctx.enter_context(nc.sbuf_tensor(name, shape, dt))

        def sem(name):
            return ctx.enter_context(nc.semaphore(name))

        bank = [ctx.enter_context(nc.psum_tensor(f"bank{i}", [P, 512], F32)) for i in range(8)]

        w1hi = sb("w1hi", [P, E * KC * HID], F32R)
        w1lo = sb("w1lo", [P, E * KC * HID], F32R)
        w2hi = sb("w2hi", [P, E * HC * D], F32R)
        w2lo = sb("w2lo", [P, E * HC * D], F32R)
        w1s = sb("w1_stage", [P, KC * HID])
        w2s = sb("w2_stage", [P, HC * D])
        ident = sb("ident", [P, P])
        upper = sb("upper", [P, P], BF16)
        ones = sb("ones", [P, P], BF16)
        tokid = sb("tokid", [P, NP // P], I32)
        far = sb("far", [P, NP // P])
        keep = sb("keep", [P, NP // P])
        iota_e = sb("iota_e", [P, E])
        region0 = sb("region0", [P, E])
        one8 = sb("one8", [P, E])
        iota_j = sb("iota_j", [1, TILES])
        padrow = sb("padrow", [P, ROW])
        wcat = sb("wcat", [P, KC, D + 2 * H])
        gatew = sb("gatew", [P, KC, E])
        gateb = sb("gateb", [P, E])
        edge = sb("edge", [P, GROUPS, 2 * GT], I32)
        edge_g = sb("edge_g", [P, 2 * GT], I32)
        turned = sb("turned", [P, RING, D])
        NODES, XTS = GT * D, GT * (D + 2 * H)
        BIASES = max(2 * NODES, NODES + GT * XW)
        shared = sb("shared", [P, max(2 * NODES + 2 * XTS, BIASES + E * HID)])
        xa = [shared[:, k * NODES:(k + 1) * NODES].rearrange("p (t d) -> p t d", t=GT) for k in range(2)]
        xt = [shared[:, 2 * NODES + k * XTS:2 * NODES + (k + 1) * XTS].rearrange("p (t d) -> p t d", t=GT)
              for k in range(2)]
        al = sb("al", [P, GROUPS, GT * H])
        xg = xa[0]
        gx = shared[:, NODES:NODES + GT * XW].rearrange("p (t d) -> p t d", t=GT)
        gal = sb("gal", [P, GT, H])
        attnl, attnr = turned[:, 0, :], turned[:, 1, :]
        rows = sb("rows", [P, GT, ROW])
        st = sb("st", [P, GT, 6])
        ln = [sb(f"ln_{i}", [P, GT]) for i in range(10)]
        sc = sb("sc", [P, GT, H])
        lr = sb("lr", [P, GT, H])
        hm = sb("hm", [P, GT])
        he = sb("he", [P, GT, H])
        hsum = sb("hsum", [P, GT])
        hrec = sb("hrec", [P, GT])
        alpha = sb("alpha", [P, GT, H])
        prod = sb("prod", [P, 2, D])
        msg = sb("msg", [P, RING, DH])
        lg = sb("lg", [P, GT, E])
        mx = sb("mx", [P, GT, 8])
        mi = sb("mi", [P, GT, 8], U32)
        mif = sb("mif", [P, GT, TOP])
        em = sb("em", [P, GT, E])
        ex = sb("ex", [P, GT, E])
        esum = sb("esum", [P, GT])
        erec = sb("erec", [P, GT])
        pr = sb("pr", [P, GT, E])
        pm = sb("pm", [P, GT, E])
        mask = sb("mask", [P, GT, TOP, E])
        both = sb("both", [P, GT, E])
        both16 = sb("both16", [P, GT, E], BF16)
        rank = sb("rank", [P, GT, E])
        mrank = sb("mrank", [P, GT, TOP, E])
        posf = sb("posf", [P, GT, TOP])
        posi = sb("posi", [P, GT, TOP], I32)
        filled = sb("filled", [P, E])
        filled_i = sb("filled_i", [1, E], I32)
        cnt = sb("cnt", [1, E])
        cnt_i = sb("cnt_i", [1, E], I32)
        nt_i = sb("nt_i", [1, E], I32)
        nt = sb("nt", [1, E])
        upto = sb("upto", [1, E])
        TE = TILES * E
        ge = w1s[0:1, 0:TE].rearrange("p (j e) -> p j e", e=E)
        gn = w2s[0:1, 0:TE].rearrange("p (j e) -> p j e", e=E)
        tf = prod[0:1, :, :].rearrange("p s d -> p (s d)")[:, 0:4 * TILES].rearrange("p (k j) -> p k j", k=4)
        ti = sb("ti", [1, 6, TILES], I32)
        hb = shared[:, 0:2 * HID].rearrange("p (s m) -> p s m", s=2)
        b2bc = shared[:, 2 * HID:2 * HID + E * D]
        assert 2 * HID + E * D <= BIASES
        yb = prod
        xin = turned[:, :, :].rearrange("p s d -> p (s d)")[:, 0:2 * ROW].rearrange("p (s m) -> p s m", s=2)
        b1bc = shared[:, BIASES:BIASES + E * HID]
        xThi = sb("xThi", [P, 2, KC * P], F32R)
        xTlo = sb("xTlo", [P, 2, KC * P], F32R)
        hThi = sb("hThi", [P, 2, HID], F32R)
        hTlo = sb("hTlo", [P, 2, HID], F32R)
        tokring = sb("tokring", [P, TILES], I32)
        cwring = sb("cwring", [P, TILES])
        toknow = sb("toknow", [P, 2], I32)

        s_edge, s_const, s_vw, s_bias = sem("s_edge"), sem("s_const"), sem("s_vw"), sem("s_bias")
        s_w, s_whi, s_wlo = sem("s_w"), sem("s_whi"), sem("s_wlo")
        s_pool, s_zero, s_fold = sem("s_pool"), sem("s_zero"), sem("s_fold")
        s_settled, s_sp_settled = sem("s_settled"), sem("s_sp_settled")
        a_in, a_store = [sem(f"a_in{i}") for i in range(2)], [sem(f"a_store{i}") for i in range(2)]
        a_norm, a_turn, a_turned, a_xt, a_out, a_al, a_steps, a_alstore = (
            sem(k) for k in ("a_norm", "a_turn", "a_turned", "a_xt", "a_out", "a_al", "a_steps", "a_alstore"))
        s_gath = [sem(f"s_gath{i}") for i in range(GT)]
        s_scat = [sem(f"s_scat{i}") for i in range(GT)]
        s_edge_g, s_steps, s_b1 = sem("s_edge_g"), sem("s_steps"), sem("s_b1")
        s_harg, s_hexp, s_alpha = sem("s_harg"), sem("s_hexp"), sem("s_alpha")
        s_prod, s_msg, s_x2, s_rstd = sem("s_prod"), sem("s_msg"), sem("s_x2"), sem("s_rstd")
        s_nr, s_nra, s_t2, s_e2, s_gate = sem("s_nr"), sem("s_nra"), sem("s_t2"), sem("s_e2"), sem("s_gate")
        s_garg, s_gexp, s_both, s_ranks = sem("s_garg"), sem("s_gexp"), sem("s_both"), sem("s_ranks")
        s_pos, s_cw = sem("s_pos"), sem("s_cw")
        s_xin, s_out = sem("s_xin"), sem("s_out")
        s_tab, s_tables, s_pads = sem("s_tab"), sem("s_tables"), sem("s_pads")
        p_xin = [sem(f"p_xin{i}") for i in range(2)]
        p_add = [sem(f"p_add{i}") for i in range(2)]
        p_xT, p_xhi, p_xlo, p_h, p_bias, p_gelu, p_hT, p_hhi, p_hlo, p_y, p_yb, p_yout, p_meta, p_tok = (
            sem(k) for k in ("p_xT", "p_xhi", "p_xlo", "p_h", "p_bias", "p_gelu", "p_hT", "p_hhi", "p_hlo", "p_y",
                             "p_yb", "p_yout", "p_meta", "p_tok"))

        block = ctx.enter_context(nc.Block())
        LAST = GROUPS - 1

        def tile_rows(dram, g):
            r = g * (GT * P)
            part = dram[r:r + GT * P, :] if isinstance(g, int) else dram[ds(r, GT * P), :]
            return part.rearrange("(p t) c -> p t c", p=P)

        def node_groups(engine, body):
            body(0, 0, 0)
            body(1, 1, 0)
            with engine.Fori(1, GROUPS // 2) as k:
                body(2 * k, 0, k)
                body(2 * k + 1, 1, k)
            body(LAST, 0, LAST // 2)

        def slot_used(g, i, ring=RING):
            return not (isinstance(g, int) and g == 0 and i < ring)

        @block.sync
        def _(sp):
            sp.dma_start(edge[:, :, :], edges).then_inc(s_edge, 16)

            def load_x(g):
                sp.dma_start(xg[:, :, :], tile_rows(x, g)).then_inc(s_xin, 16)

            def load_expert(e):
                a = w1[e:e + 1] if isinstance(e, int) else w1[ds(e, 1)]
                b = w2[e:e + 1] if isinstance(e, int) else w2[ds(e, 1)]
                sp.dma_start(w1s[:, :].rearrange("p (c m) -> p c m", c=KC),
                             a.rearrange("e (c p) m -> p (e c) m", p=P)).then_inc(s_w, 16)
                sp.dma_start(w2s[:, :].rearrange("p (c m) -> p c m", c=HC),
                             b.rearrange("e (c p) m -> p (e c) m", p=P)).then_inc(s_w, 16)

            sp.dma_start(wcat[:, :, 0:D], gw.rearrange("(c p) m -> p c m", p=P)).then_inc(s_vw, 16)
            sp.dma_start(attnl[:, :], attn_l.rearrange("h d -> (h d)").partition_broadcast(P)).then_inc(s_vw, 16)
            sp.dma_start(attnr[:, :], attn_r.rearrange("h d -> (h d)").partition_broadcast(P)).then_inc(s_vw, 16)
            sp.dma_start(xa[0], tile_rows(x, 0)).then_inc(a_in[0], 16)
            sp.dma_start(xa[1], tile_rows(x, 1)).then_inc(a_in[1], 16)
            load_expert(0)
            sp.dma_start(gatew[:, :, :], gate_w.rearrange("(c p) m -> p c m", p=P)).then_inc(s_bias, 16)
            sp.dma_start(gateb[:, :], gate_b.partition_broadcast(P)).then_inc(s_bias, 16)

            def settle():
                sp.sem_inc(s_sp_settled, 1)

            def a_group(g, s, h):
                if not (isinstance(g, int) and g + 2 >= GROUPS):
                    sp.wait_ge(a_turn, GT * (g + 1))
                    sp.dma_start(xa[s], tile_rows(x, g + 2)).then_inc(a_in[s], 16)
                sp.wait_ge(a_out, GT * (g + 1))
                sp.dma_start(tile_rows(table, g), xt[s][:, :, 0:XW]).then_inc(a_store[s], 16)

            a_group(0, 0, 0)
            a_group(1, 1, 0)
            with sp.Fori(1, GROUPS // 2 - 1) as k:
                a_group(2 * k, 0, k)
                a_group(2 * k + 1, 1, k)
            for g in range(GROUPS - GROUPS % 2 - 2, GROUPS):
                a_group(g, g % 2, g // 2)
            sp.wait_ge(a_al, GROUPS)
            sp.dma_start(src_scores.rearrange("(g p t) h -> p g (t h)", g=GROUPS, p=P), al[:, :, :]
                         ).then_inc(a_alstore, 16)
            load_x(0)

            def group(g, last):
                if isinstance(g, int) and g == 0:
                    for s in range(2):
                        sp.wait_ge(a_store[s], 16 * ((GROUPS + 1 - s) // 2))
                    sp.dma_start(b1bc, b1.rearrange("e m -> (e m)").partition_broadcast(P)).then_inc(s_b1, 16)
                sp.wait_ge(s_wlo, 2 * (g + 1))
                load_expert(g + 1)
                sp.wait_ge(s_x2, GT * (g + 1))
                sp.dma_start(tile_rows(out, g), xg[:, :, :]).then_inc(s_out, 16)
                if not last:
                    sp.wait_ge(s_out, 16 * (g + 1))
                    settle()
                    sp.wait_ge(s_nr, ND * (g + 1))
                    settle()
                    sp.wait_ge(s_nra, (GT - ND) * (g + 1))
                    load_x(g + 1)

            group(0, False)
            with sp.Fori(1, LAST) as g:
                group(g, False)
            group(LAST, True)

            sp.wait_ge(s_out, 16 * GROUPS)
            sp.wait_ge(s_tables, 1)
            sp.dma_start(b2bc, b2.rearrange("e m -> (e m)").partition_broadcast(P)).then_inc(s_b1, 16)
            sp.wait_ge(s_pool, 1)
            for e in range(E):
                r = sp.value_load(filled_i[0:1, e:e + 1], min_val=e * CAP, max_val=e * CAP + NP)
                sp.dma_start(xs[ds(r, P), :], padrow[:, :]).then_inc(s_pads, 16)
            sp.wait_ge(s_pads, 16 * E)
            sp.wait_ge(s_zero, ZEROS)
            for i in range(GT):
                sp.wait_ge(s_scat[i], 32 * GROUPS)

            def load_tile(j, s, fresh):
                if not fresh:
                    sp.wait_ge(p_xT, j - 1)
                    sp.wait_ge(p_meta, j - 1)
                r = sp.value_load(ti[0:1, 1, ds(j, 1)], min_val=0, max_val=XS_ROWS - P)
                sp.dma_start(xin[:, s, :], xs[ds(r, P), :]).then_inc(p_xin[s], 16)

            load_tile(0, 0, True)
            load_tile(1, 1, True)
            with sp.Fori(1, TILES // 2) as k:
                load_tile(2 * k, 0, False)
                load_tile(2 * k + 1, 1, False)

        @block.gpsimd
        def _(pool):
            pool.memset(rows[:, :, :], 0.0).then_inc(s_const, 1)
            pool.memset(padrow[:, :], 0.0).then_inc(s_const, 1)
            pool.memset(ident[:, :], 0.0).then_inc(s_const, 1)
            pool.memset(upper[:, :], 1.0).then_inc(s_const, 1)
            pool.memset(ones[:, :], 1.0).then_inc(s_const, 1)
            pool.memset(one8[:, :], 1.0).then_inc(s_const, 1)
            pool.iota(tokid[:, :], [[P * GT, GROUPS], [1, GT]], base=0, channel_multiplier=GT).then_inc(s_const, 1)
            pool.memset(keep[:, :], 1.0).then_inc(s_const, 1)
            pool.memset(far[:, :], 0.0).then_inc(s_const, 1)
            pool.iota(iota_e[:, :], [[1, E]], base=0, channel_multiplier=0,
                      allow_small_or_imprecise_dtypes=True).then_inc(s_const, 1)
            pool.iota(region0[:, :], [[CAP, E]], base=0, channel_multiplier=0,
                      allow_small_or_imprecise_dtypes=True).then_inc(s_const, 1)
            pool.iota(filled[:, :], [[CAP, E]], base=0, channel_multiplier=0,
                      allow_small_or_imprecise_dtypes=True).then_inc(s_const, 1)
            pool.iota(iota_j[:, :], [[1, TILES]], base=0, channel_multiplier=0,
                      allow_small_or_imprecise_dtypes=True).then_inc(s_const, 1)
            pool.wait_ge(s_const, 13)
            pool.affine_select(ident[:, :], ident[:, :], [[1, P]], ALU.not_equal, 1.0, base=0,
                               channel_multiplier=-1).then_inc(s_const, 1)
            pool.affine_select(upper[:, :], upper[:, :], [[1, P]], ALU.is_gt, 0.0, base=0,
                               channel_multiplier=-1).then_inc(s_const, 1)
            pool.affine_select(keep[:, :], keep[:, :], [[-P * GT, GROUPS], [-1, GT]], ALU.is_gt, 0.0, base=n,
                               channel_multiplier=-GT).then_inc(s_const, 1)
            pool.affine_select(far[:, :], far[:, :], [[-P * GT, GROUPS], [-1, GT]], ALU.is_gt, FAR, base=n,
                               channel_multiplier=-GT).then_inc(s_const, 1)
            pool.iota(rows[:, :, TOK:TOK + 1].bitcast(I32), [[P, GT], [1, 1]], base=NP,
                      channel_multiplier=1).then_inc(s_const, 1)
            pool.iota(padrow[:, TOK:TOK + 1].bitcast(I32), [[1, 1]], base=NP, channel_multiplier=1).then_inc(s_pool, 1)
            pool.wait_ge(s_edge, 16)

            def settle():
                pool.sem_inc(s_settled, 1)

            def gathers(g, first):
                if not first:
                    for i in range(GT):
                        pool.wait_ge(s_gath[i], 32 * g)
                at = edge[:, g, :] if isinstance(g, int) else edge[:, ds(g, 1), :].rearrange("p a t -> p (a t)")
                pool.tensor_copy(edge_g[:, :], at).then_inc(s_edge_g, 1)
                pool.wait_ge(s_edge_g, g + 1)
                for i in range(GT):
                    if not first:
                        pool.wait_ge(s_prod, GT * (g - 1) + i + 1)
                    settle()
                    pool.indirect_dma_start(gx[:, i, :], None, table,
                                            bass.IndirectOffsetOnAxis(edge_g[:, i:i + 1], 0)).then_inc(s_gath[i], 16)
                    pool.indirect_dma_start(gal[:, i, :], None, src_scores,
                                            bass.IndirectOffsetOnAxis(edge_g[:, GT + i:GT + i + 1], 0)
                                            ).then_inc(s_gath[i], 16)

            def scatters(g):
                pool.wait_ge(s_pos, g + 1)
                settle()
                for i in range(GT):
                    for k in range(TOP):
                        pool.indirect_dma_start(xs, bass.IndirectOffsetOnAxis(posi[:, i, k:k + 1], 0), rows[:, i, :],
                                                None, bounds_check=XS_ROWS - 1, oob_is_err=False
                                                ).then_inc(s_scat[i], 16)

            pool.wait_ge(s_const, 18)
            for t0 in range(0, DUMMIES, GT):
                m = min(GT, DUMMIES - t0)
                pool.dma_start(xs[E * CAP + t0 * P:E * CAP + (t0 + m) * P, :].rearrange("(t p) c -> p t c", p=P),
                               rows[:, 0:m, :]).then_inc(s_zero, 16)
            for t0 in range(0, 1 + DUMMIES, GT):
                m = min(GT, 1 + DUMMIES - t0)
                pool.dma_start(out[NP + t0 * P:NP + (t0 + m) * P, :].rearrange("(t p) c -> p t c", p=P),
                               rows[:, 0:m, 0:D]).then_inc(s_zero, 16)
            def set_apart(g, s, h):
                pool.wait_ge(a_out, GT * (g + 1))
                pool.tensor_copy(al[:, g, :].rearrange("p (t h) -> p t h", t=GT) if isinstance(g, int)
                                 else al[:, ds(g, 1), :].rearrange("p a (t h) -> p (a t) h", t=GT),
                                 xt[s][:, :, XW:XW + H]).then_inc(a_al, 1)

            node_groups(pool, set_apart)
            for s in range(2):
                pool.wait_ge(a_store[s], 16 * ((GROUPS + 1 - s) // 2))
            pool.wait_ge(a_alstore, 16)
            gathers(0, True)
            gathers(1, False)
            scatters(0)
            with pool.Fori(1, LAST) as g:
                gathers(g + 1, False)
                scatters(g)
            scatters(LAST)

            pool.wait_ge(s_tables, 1)
            pool.wait_ge(s_out, 16 * GROUPS)
            pool.wait_ge(s_zero, ZEROS)

            def keep_meta(j, s):
                pool.wait_ge(p_xin[s], 16 * (half(j) + 1))
                settle()
                e = pool.value_load(ti[0:1, 0, ds(j, 1)], min_val=0, max_val=E - 1)
                pool.tensor_copy(cwring[:, ds(j, 1)], xin[:, s, ds(e + CW, 1)])
                pool.tensor_copy(tokring[:, ds(j, 1)], xin[:, s, TOK:TOK + 1].bitcast(I32)).then_inc(p_meta, 1)

            def half(j):
                return j // 2 if isinstance(j, int) else j >> 1

            def add_tile(j, s):
                first = isinstance(j, int) and j < 2
                if not first:
                    pool.wait_ge(p_add[s], 16 * half(j))
                pool.wait_ge(p_meta, j + 1)
                pool.tensor_copy(toknow[:, s:s + 1], tokring[:, ds(j, 1)]).then_inc(p_tok, 1)
                pool.wait_ge(p_tok, j + 1)
                for q in range(2):
                    if not first or (q == 0 and j == 1):
                        settle()
                        before = pool.value_load(ti[0:1, 2 + q, ds(j, 1)], min_val=16, max_val=16 * TILES)
                        pool.wait_ge(p_add[q], before)
                pool.wait_ge(p_yout, j + 1)
                settle()
                pool.indirect_dma_start(out, bass.IndirectOffsetOnAxis(toknow[:, s:s + 1], 0), yb[:, s, :], None,
                                        compute_op=ALU.add).then_inc(p_add[s], 16)

            keep_meta(0, 0)
            keep_meta(1, 1)
            for s in range(2):
                keep_meta(2 + s, s)
                add_tile(s, s)
            with pool.Fori(1, TILES // 2 - 1) as k:
                for s in range(2):
                    keep_meta(2 * k + 2 + s, s)
                    add_tile(2 * k + s, s)
            for s in range(2):
                add_tile(TILES - 2 + s, s)
            for s in range(2):
                pool.wait_ge(p_add[s], 16 * (TILES // 2))

        @block.scalar
        def _(act):
            def split_high(e):
                act.wait_ge(s_w, 32 * (e + 1))
                act.activation(w1hi[:, ds(e * (KC * HID), KC * HID)], w1s[:, :], ACT.Copy).then_inc(s_whi, 1)
                act.activation(w2hi[:, ds(e * (HC * D), HC * D)], w2s[:, :], ACT.Copy).then_inc(s_whi, 1)

            split_high(0)

            def a_group(g, s, h):
                def turned_out(i):
                    n_tile = GT * g + i + 1
                    act.wait_ge(a_turn, n_tile)
                    if slot_used(g, i):
                        act.wait_ge(a_xt, n_tile - back(i))
                    act.activation(turned[:, i % RING, :], bank[i % RING][:, 0:D], ACT.Copy).then_inc(a_turned, 1)

                def product_out(i):
                    act.wait_ge(a_xt, GT * g + i + 1)
                    act.activation(xt[s][:, i, :], bank[RING + i % RING][:, 0:D + 2 * H], ACT.Copy).then_inc(a_out, 1)

                for i in range(GT):
                    turned_out(i)
                    if i == 1 and not (isinstance(g, int) and g < 2):
                        act.wait_ge(a_store[s], 16 * h)
                        act.wait_ge(a_al, g - 1)
                    if i:
                        product_out(i - 1)
                product_out(GT - 1)

            node_groups(act, a_group)

            def group(g):
                first = isinstance(g, int) and g == 0
                split_high(g + 1)
                act.wait_ge(s_harg, g + 1)
                act.activation(he[:, :, :], he[:, :, :], ACT.Exp).then_inc(s_hexp, 1)
                act.wait_ge(s_alpha, g + 1)
                for i in range(GT):
                    if slot_used(g, i, 2):
                        act.wait_ge(s_msg, GT * g + i + 1 - back(i, 2))
                    for k in range(H):
                        at = slice(k * DH, (k + 1) * DH)
                        ins = act.activation(prod[:, i % 2, at], gx[:, i, at], ACT.Copy, scale=alpha[:, i, k:k + 1])
                    ins.then_inc(s_prod, 1)
                act.wait_ge(s_rstd, g + 1)
                if first:
                    act.wait_ge(s_zero, ZEROS)

                def turned_out(i):
                    act.wait_ge(s_t2, GT * g + i + 1)
                    if slot_used(g, i):
                        act.wait_ge(s_gate, GT * g + i + 1 - back(i))
                    act.activation(turned[:, i % RING, :], bank[i % RING][:, 0:D], ACT.Copy).then_inc(s_e2, 1)

                for i in range(ND, GT):
                    if not first:
                        act.wait_ge(s_scat[i], 32 * g)
                    act.activation(rows[:, i, 0:D], xg[:, i, :], ACT.Identity, bias=ln[8][:, i:i + 1],
                                   scale=ln[6][:, i:i + 1]).then_inc(s_nra, 1)
                    turned_out(i - ND)
                for i in range(GT - ND, GT):
                    turned_out(i)
                act.wait_ge(s_garg, g + 1)
                act.activation(ex[:, :, :], em[:, :, :], ACT.Exp).then_inc(s_gexp, 1)

            group(0)
            with act.Fori(1, GROUPS) as g:
                group(g)

            def half(j):
                return j // 2 if isinstance(j, int) else j >> 1

            def x_high(j, s):
                act.wait_ge(p_xT, j + 1)
                if not isinstance(j, int) or j >= 2:
                    act.wait_ge(p_h, j - 1)
                act.activation(xThi[:, s, :], bank[0][:, 0:D], ACT.Copy).then_inc(p_xhi, 1)

            def gelu(j, s):
                act.wait_ge(p_bias, j + 1)
                act.activation(hb[:, s, :], hb[:, s, :], ACT.Gelu).then_inc(p_gelu, 1)

            def h_high(j, s):
                act.wait_ge(p_hT, j + 1)
                if not isinstance(j, int) or j >= 2:
                    act.wait_ge(p_y, j - 1)
                act.activation(hThi[:, s, :], bank[3 + s][:, :], ACT.Copy).then_inc(p_hhi, 1)

            def y_out(j, s):
                act.wait_ge(p_yb, j + 1)
                act.wait_ge(p_meta, j + 1)
                act.activation(yb[:, s, :], yb[:, s, :], ACT.Copy, scale=cwring[:, ds(j, 1)]).then_inc(p_yout, 1)

            x_high(0, 0)
            gelu(0, 0)
            x_high(1, 1)

            def step(j, s):
                if not (isinstance(j, int) and j + 1 >= TILES):
                    x_high(j + 1, 1 - s)
                gelu(j, s)
                h_high(j - 1, 1 - s)
                if not isinstance(j, int) or j >= 2:
                    y_out(j - 2, s)

            step(1, 1)
            step(2, 0)
            step(3, 1)
            with act.Fori(2, TILES // 2 - 1) as k:
                step(2 * k, 0)
                step(2 * k + 1, 1)
            step(TILES - 2, 0)
            step(TILES - 1, 1)
            y_out(TILES - 2, 0)
            h_high(TILES - 1, 1)
            y_out(TILES - 1, 1)

        @block.vector
        def _(dve):
            def split_low(e, which):
                at = ds(e * (KC * HID), KC * HID)
                hi, lo, stage = ((w1hi, w1lo, w1s), (w2hi, w2lo, w2s))[which]
                dve.wait_ge(s_whi, 2 * e + 1 + which)
                dve.tensor_tensor(lo[:, at], stage[:, :], hi[:, at].bitcast(F32), ALU.subtract).then_inc(s_wlo, 1)

            dve.wait_ge(s_vw, 48)
            fold = Steps(dve, s_fold)
            for a, at in ((attnr, D), (attnl, D + H)):
                fold.did(dve.tensor_tensor(prod[:, 0:KC, :], wcat[:, :, 0:D],
                                           a.unsqueeze(1).to_broadcast([P, KC, D]), ALU.mult))
                fold.wait()
                fold.did(dve.tensor_reduce(wcat[:, :, at:at + H],
                                           prod[:, 0:KC, :].rearrange("p c (h d) -> p c h d", h=H), AX.X, ALU.add))
                fold.wait()
            FOLDS = fold.n
            assert FOLDS == N_FOLD
            dve.wait_ge(s_const, 18)

            def variance(t):
                msum, md, vs, mean, md2, vs2, veps = (ln[k][:, :] for k in (0, 1, 2, 3, 4, 9, 5))
                dve.tensor_tensor(vs, st[:, :, 2], st[:, :, 5], ALU.add)
                t.did(dve.tensor_tensor(md, st[:, :, 1], st[:, :, 4], ALU.subtract))
                dve.tensor_tensor(msum, st[:, :, 1], st[:, :, 4], ALU.add)
                t.wait()
                t.did(dve.tensor_tensor(md2, md, md, ALU.mult))
                t.did(dve.tensor_scalar(vs2, vs, 1.0 / D, EPS, ALU.mult, ALU.add))
                t.wait()
                t.did(dve.scalar_tensor_tensor(veps, md2, 0.25, vs2, ALU.mult, ALU.add))
                t.did(dve.tensor_scalar(mean, msum, 0.5, None, ALU.mult))
                t.wait()

            def rstd(t):
                minus_half, square, part_, veps, guess, r = (ln[k] for k in (1, 2, 4, 5, 6, 7))
                t.did(dve.tensor_scalar(guess[:, :].bitcast(I32), veps[:, :].bitcast(I32), 1, None,
                                        ALU.logical_shift_right))
                dve.tensor_scalar(minus_half[:, :], veps[:, :], -0.5, None, ALU.mult)
                t.wait()
                t.did(dve.tensor_scalar(r[:, :].bitcast(I32), guess[:, :].bitcast(I32), -1.0, GUESS, ALU.mult, ALU.add))
                t.wait()
                for step in range(3):
                    y, refined = (r, guess) if step % 2 == 0 else (guess, r)
                    t.did(dve.tensor_tensor(square[:, :], y[:, :], y[:, :], ALU.mult))
                    t.wait()
                    t.did(dve.tensor_tensor(part_[:, :], square[:, :], minus_half[:, :], ALU.mult))
                    t.wait()
                    t.did(dve.scalar_tensor_tensor(refined[:, :], part_[:, :], 1.5, y[:, :], ALU.add, ALU.mult))
                    t.wait()

            ta = Steps(dve, a_steps, A_STEPS)

            def a_group(g, s, h):
                dve.wait_ge(a_in[s], 16 * (h + 1))
                for i in range(GT):
                    ins = dve.bn_stats(st[:, i, :], xa[s][:, i, :])
                ta.begin(g)
                ta.did(ins)
                ta.wait()
                if not (isinstance(g, int) and g == 0):
                    dve.wait_ge(a_norm, GT * g)
                variance(ta)
                rstd(ta)
                for i in range(GT):
                    dve.tensor_scalar(xa[s][:, i, :], xa[s][:, i, :], ln[3][:, i:i + 1], ln[6][:, i:i + 1],
                                      ALU.subtract, ALU.mult).then_inc(a_norm, 1)
                ta.end()
                if isinstance(g, int) and g == 1:
                    split_low(0, 0)
                    split_low(0, 1)

            node_groups(dve, a_group)

            t = Steps(dve, s_steps, B_STEPS)

            def group(g):
                first = isinstance(g, int) and g == 0
                t.begin(g)
                for i in range(GT):
                    dve.wait_ge(s_gath[i], 32 * (g + 1))
                t.did(dve.tensor_tensor(sc[:, :, :], gx[:, :, D:XW], gal[:, :, :], ALU.add))
                t.wait()
                t.did(dve.scalar_tensor_tensor(lr[:, :, :], sc[:, :, :], SLOPE, sc[:, :, :], ALU.mult, ALU.max))
                t.wait()
                t.did(dve.tensor_reduce(hm[:, :], lr[:, :, :], AX.X, ALU.max))
                t.wait()
                dve.tensor_tensor(he[:, :, :], lr[:, :, :], hm[:, :].unsqueeze(2).to_broadcast([P, GT, H]),
                                  ALU.subtract).then_inc(s_harg, 1)
                dve.wait_ge(s_hexp, g + 1)
                t.did(dve.tensor_reduce(hsum[:, :], he[:, :, :], AX.X, ALU.add))
                t.wait()
                t.did(dve.reciprocal(hrec[:, :], hsum[:, :]))
                t.wait()
                dve.tensor_tensor(alpha[:, :, :], he[:, :, :], hrec[:, :].unsqueeze(2).to_broadcast([P, GT, H]),
                                  ALU.mult).then_inc(s_alpha, 1)
                dve.wait_ge(s_xin, 16 * (g + 1))

                def heads(i):
                    dve.wait_ge(s_prod, GT * g + i + 1)
                    dve.tensor_reduce(msg[:, i % RING, :], prod[:, i % 2, :].rearrange("p (h d) -> p d h", h=H),
                                      AX.X, ALU.add).then_inc(s_msg, 1)

                def residual(i):
                    dve.wait_ge(s_msg, GT * g + i + 1)
                    xv = xg[:, i, :].rearrange("p (h d) -> p h d", h=H)
                    dve.tensor_tensor(xv, xv, msg[:, i % RING, :].unsqueeze(1).to_broadcast([P, H, DH]), ALU.add
                                      ).then_inc(s_x2, 1)

                for i in range(GT + 2):
                    if i < GT:
                        heads(i)
                    if 1 <= i <= GT:
                        residual(i - 1)
                    if i >= 2:
                        dve.wait_ge(s_x2, GT * g + i - 1)
                        ins = dve.bn_stats(st[:, i - 2, :], xg[:, i - 2, :])
                t.did(ins)
                t.wait()
                variance(t)
                rstd(t)
                dve.scalar_tensor_tensor(ln[8][:, :], ln[3][:, :], -1.0, ln[6][:, :], ALU.mult, ALU.mult
                                         ).then_inc(s_rstd, 1)
                if first:
                    dve.wait_ge(s_zero, ZEROS)
                for i in range(GT):
                    if not first:
                        dve.wait_ge(s_scat[i], 32 * g)
                    if i < ND:
                        dve.tensor_scalar(rows[:, i, 0:D], xg[:, i, :], ln[3][:, i:i + 1], ln[6][:, i:i + 1],
                                          ALU.subtract, ALU.mult).then_inc(s_nr, 1)
                split_low(g + 1, 0)
                at = ds(g * GT, GT)
                dve.wait_ge(s_gate, GT * (g + 1))
                t.did(dve.tensor_tensor(lg[:, :, :], bank[5][:, 0:GT * E].rearrange("p (t e) -> p t e", e=E),
                                        gateb[:, :].unsqueeze(1).to_broadcast([P, GT, E]), ALU.add))
                t.wait()
                dve.tensor_copy(rows[:, 0:GT, TOK].bitcast(I32), tokid[:, at])
                for i in range(GT):
                    ins = dve.max(mx[:, i, :], lg[:, i, :])
                t.did(ins)
                t.wait()
                dve.tensor_tensor(em[:, :, :], lg[:, :, :], mx[:, :, 0:1].to_broadcast([P, GT, E]),
                                  ALU.subtract).then_inc(s_garg, 1)
                for i in range(GT):
                    ins = dve.max_index(mi[:, i, :], mx[:, i, :], lg[:, i, :])
                t.did(ins)
                t.wait()
                t.did(dve.tensor_copy(mif[:, :, :], mi[:, :, 0:TOP]))
                t.wait()
                t.did(dve.tensor_tensor(mask[:, :, :, :], mif[:, :, :].unsqueeze(3).to_broadcast([P, GT, TOP, E]),
                                        iota_e[:, :].unsqueeze(1).unsqueeze(1).to_broadcast([P, GT, TOP, E]),
                                        ALU.is_equal))
                t.wait()
                t.did(dve.tensor_tensor(both[:, :, :], mask[:, :, 0, :], mask[:, :, 1, :], ALU.add))
                t.wait()
                dve.tensor_tensor(both16[:, :, :], both[:, :, :], keep[:, at].unsqueeze(2).to_broadcast([P, GT, E]),
                                  ALU.mult).then_inc(s_both, 1)
                split_low(g + 1, 1)
                dve.wait_ge(s_gexp, g + 1)
                dve.tensor_tensor(pr[:, :, :], ex[:, :, :], both[:, :, :], ALU.mult)
                t.did(dve.tensor_reduce(esum[:, :], ex[:, :, :], AX.X, ALU.add))
                t.wait()
                t.did(dve.reciprocal(erec[:, :], esum[:, :]))
                t.wait()
                dve.tensor_tensor(rows[:, 0:GT, CW:ROW], pr[:, :, :], erec[:, :].unsqueeze(2).to_broadcast([P, GT, E]),
                                  ALU.mult).then_inc(s_cw, 1)
                dve.wait_ge(s_ranks, g + 1)
                t.did(dve.tensor_tensor(rank[:, :, :], bank[6][:, 0:GT * E].rearrange("p (t e) -> p t e", e=E),
                                        filled[:, :].unsqueeze(1).to_broadcast([P, GT, E]), ALU.add))
                t.wait()
                dve.tensor_tensor(filled[:, :], bank[6][:, 64:64 + E], filled[:, :], ALU.add)
                t.did(dve.tensor_tensor(mrank[:, :, :, :], mask[:, :, :, :],
                                        rank[:, :, :].unsqueeze(2).to_broadcast([P, GT, TOP, E]), ALU.mult))
                t.wait()
                t.did(dve.tensor_reduce(posf[:, :, :], mrank[:, :, :, :], AX.X, ALU.add))
                t.wait()
                dve.tensor_tensor(posi[:, :, :], posf[:, :, :], far[:, at].unsqueeze(2).to_broadcast([P, GT, TOP]),
                                  ALU.add).then_inc(s_pos, 1)
                t.end()

            group(0)
            with dve.Fori(1, GROUPS) as g:
                group(g)

            u = Steps(dve, s_tab)
            dve.wait_ge(s_wlo, 2 * E)
            dve.tensor_copy(filled_i[:, :], filled[0:1, :])
            u.did(dve.tensor_tensor(cnt[:, :], filled[0:1, :], region0[0:1, :], ALU.subtract))
            u.wait()
            u.did(dve.tensor_scalar(cnt_i[:, :], cnt[:, :], float(P - 1), None, ALU.add))
            u.wait()
            u.did(dve.tensor_scalar(nt_i[:, :], cnt_i[:, :], P.bit_length() - 1, None, ALU.logical_shift_right))
            u.wait()
            u.did(dve.tensor_copy(nt[:, :], nt_i[:, :]))
            u.wait()
            u.did(dve.tensor_tensor_scan(upto[:, :], one8[0:1, :], nt[:, :], 0.0, ALU.mult, ALU.add))
            u.wait()
            u.did(dve.tensor_tensor(ge[:, :, :], iota_j[:, :].unsqueeze(2).to_broadcast([1, TILES, E]),
                                    upto[:, :].unsqueeze(1).to_broadcast([1, TILES, E]), ALU.is_ge))
            u.wait()
            u.did(dve.tensor_tensor(gn[:, :, :], ge[:, :, :], nt[:, :].unsqueeze(1).to_broadcast([1, TILES, E]),
                                    ALU.mult))
            u.did(dve.tensor_reduce(tf[:, 0, :], ge[:, :, :], AX.X, ALU.add))
            u.wait()
            u.did(dve.tensor_reduce(tf[:, 1, :], gn[:, :, :], AX.X, ALU.add))
            dve.tensor_scalar(ti[:, 0, :], tf[:, 0, :], float(E - 1), None, ALU.min)
            u.wait()
            u.did(dve.tensor_tensor(tf[:, 2, :], iota_j[:, :], tf[:, 1, :], ALU.subtract))
            u.did(dve.tensor_copy(ti[:, 4, :], tf[:, 1, :]))
            u.wait()
            u.did(dve.tensor_scalar(tf[:, 3, :], tf[:, 0, :], float(CAP), None, ALU.mult))
            u.did(dve.tensor_scalar(ti[:, 5, :], tf[:, 1, :], 1.0, None, ALU.add))
            u.wait()
            dve.scalar_tensor_tensor(ti[:, 1, :], tf[:, 2, :], float(P), tf[:, 3, :], ALU.mult, ALU.add)
            u.did(dve.tensor_scalar(ti[:, 4:6, :], ti[:, 4:6, :], 1, None, ALU.logical_shift_right))
            u.wait()
            u.did(dve.tensor_scalar(ti[:, 2, :], ti[:, 5, :], 16.0, 16.0, ALU.mult, ALU.max))
            dve.tensor_scalar(ti[:, 3, :], ti[:, 4, :], 16.0, 16.0, ALU.mult, ALU.max).then_inc(s_tables, 1)

            def expert(j):
                return dve.value_load(ti[0:1, 0, ds(j, 1)], min_val=0, max_val=E - 1)

            def add_bias1(j, s, e):
                dve.wait_ge(p_h, j + 1)
                if not isinstance(j, int) or j >= 2:
                    dve.wait_ge(p_hT, j - 1)
                dve.tensor_tensor(hb[:, s, :], bank[1 + s][:, :], b1bc[:, ds(e * HID, HID)],
                                  ALU.add).then_inc(p_bias, 1)

            def add_bias2(j, s, e, first):
                dve.wait_ge(p_y, j + 1)
                if not first:
                    dve.wait_ge(p_add[s], 16 * half(j))
                dve.tensor_tensor(yb[:, s, :], bank[5 + s][:, 0:D], b2bc[:, ds(e * D, D)], ALU.add).then_inc(p_yb, 1)

            def x_low(j, s):
                dve.wait_ge(p_xhi, j + 1)
                dve.tensor_tensor(xTlo[:, s, :], bank[0][:, 0:D], xThi[:, s, :].bitcast(F32),
                                  ALU.subtract).then_inc(p_xlo, 1)

            def h_low(j, s):
                dve.wait_ge(p_hhi, j + 1)
                dve.tensor_tensor(hTlo[:, s, :], bank[3 + s][:, :], hThi[:, s, :].bitcast(F32),
                                  ALU.subtract).then_inc(p_hlo, 1)

            def half(j):
                return j // 2 if isinstance(j, int) else j >> 1

            dve.wait_ge(s_b1, 32)
            x_low(0, 0)
            add_bias1(0, 0, expert(0))
            x_low(1, 1)

            def step(j, s, e, load_next=True):
                add_bias1(j, s, e)
                start = isinstance(j, int) and j < 2
                e_back = None if start else expert(j - 2)
                if not (isinstance(j, int) and j + 1 >= TILES):
                    x_low(j + 1, 1 - s)
                if not start:
                    add_bias2(j - 2, s, e_back, isinstance(j, int) and j < 4)
                e_next = expert(j + 1) if load_next else None
                h_low(j - 1, 1 - s)
                return e_next

            e = step(1, 1, expert(1))
            e = step(2, 0, e)
            step(3, 1, e, False)
            with dve.Fori(2, TILES // 2 - 1) as k:
                e = step(2 * k, 0, expert(2 * k))
                step(2 * k + 1, 1, e, False)
            e = step(TILES - 2, 0, expert(TILES - 2))
            step(TILES - 1, 1, e, False)
            e = expert(TILES - 2)
            add_bias2(TILES - 2, 0, e, False)
            e = expert(TILES - 1)
            h_low(TILES - 1, 1)
            add_bias2(TILES - 1, 1, e, False)

        @block.tensor
        def _(pe):
            pe.wait_ge(s_const, 18)
            pe.wait_ge(s_fold, N_FOLD)
            pe.wait_ge(s_bias, 32)

            def transpose_pair(to, src):
                for c in range(KC):
                    ins = pe.transpose(to[:, c * P:(c + 1) * P], src[:, c * P:(c + 1) * P], ident[:, :])
                return ins

            def a_group(g, s, h):
                def product(i):
                    pe.wait_ge(a_turned, GT * g + i + 1)
                    if slot_used(g, i):
                        pe.wait_ge(a_out, GT * g + i + 1 - back(i))
                    for c in range(KC):
                        ins = pe.matmul(bank[RING + i % RING][:, 0:D + 2 * H], turned[:, i % RING, c * P:(c + 1) * P],
                                        wcat[:, c, :], start=c == 0, stop=c == KC - 1)
                    ins.then_inc(a_xt, 1)

                for i in range(GT):
                    pe.wait_ge(a_norm, GT * g + i + 1)
                    if slot_used(g, i):
                        pe.wait_ge(a_turned, GT * g + i + 1 - back(i))
                    transpose_pair(bank[i % RING], xa[s][:, i, :]).then_inc(a_turn, 1)
                    if i:
                        product(i - 1)
                product(GT - 1)

            node_groups(pe, a_group)

            def gate(g, i):
                pe.wait_ge(s_e2, GT * g + i + 1)
                for c in range(KC):
                    ins = pe.matmul(bank[5][:, i * E:(i + 1) * E], turned[:, i % RING, c * P:(c + 1) * P],
                                    gatew[:, c, :], start=c == 0, stop=c == KC - 1)
                ins.then_inc(s_gate, 1)

            def group(g):
                for i in range(GT):
                    if i < ND:
                        pe.wait_ge(s_nr, ND * g + i + 1)
                    else:
                        pe.wait_ge(s_nra, (GT - ND) * g + i - ND + 1)
                    if slot_used(g, i):
                        pe.wait_ge(s_e2, GT * g + i + 1 - back(i))
                    transpose_pair(bank[i % RING], rows[:, i, 0:D]).then_inc(s_t2, 1)
                    if i:
                        gate(g, i - 1)
                gate(g, GT - 1)
                pe.wait_ge(s_both, g + 1)
                r = bank[6][:, 0:GT * E].rearrange("p (t e) -> p t e", e=E)
                pe.matmul(r, upper[:, :], both16[:, :, :], start=True, stop=False)
                for i in range(GT - 1):
                    m = GT - 1 - i
                    pe.matmul(r[:, i + 1:GT, :], ones[:, :], both16[:, i:i + 1, :].to_broadcast([P, m, E]),
                              start=False, stop=i == GT - 2)
                for i in range(GT):
                    ins = pe.matmul(bank[6][:, 64:64 + E], ones[:, :], both16[:, i, :], start=i == 0, stop=i == GT - 1)
                ins.then_inc(s_ranks, 1)

            group(0)
            with pe.Fori(1, GROUPS) as g:
                group(g)

            def half(j):
                return j // 2 if isinstance(j, int) else j >> 1

            def turn_x(j, s):
                pe.wait_ge(p_xin[s], 16 * (half(j) + 1))
                if not isinstance(j, int) or j >= 1:
                    pe.wait_ge(p_xlo, j)
                transpose_pair(bank[0], xin[:, s, 0:D]).then_inc(p_xT, 1)

            def first_product(j, s, e):
                pe.wait_ge(p_xhi, j + 1)
                o = bank[1 + s][:, :]
                for c in range(KC):
                    lhs = xThi[:, s, c * P:(c + 1) * P]
                    at = ds(e * (KC * HID) + c * HID, HID)
                    pe.matmul(o, lhs, w1hi[:, at], start=c == 0, stop=False)
                    pe.matmul(o, lhs, w1lo[:, at], start=False, stop=False)
                pe.wait_ge(p_xlo, j + 1)
                for c in range(KC):
                    at = ds(e * (KC * HID) + c * HID, HID)
                    ins = pe.matmul(o, xTlo[:, s, c * P:(c + 1) * P], w1hi[:, at], start=False, stop=c == KC - 1)
                ins.then_inc(p_h, 1)

            def turn_h(j, s):
                pe.wait_ge(p_gelu, j + 1)
                for c in range(HC):
                    ins = pe.transpose(bank[3 + s][:, c * P:(c + 1) * P], hb[:, s, c * P:(c + 1) * P], ident[:, :])
                ins.then_inc(p_hT, 1)

            def second_product(j, s, e):
                pe.wait_ge(p_hhi, j + 1)
                if not isinstance(j, int) or j >= 2:
                    pe.wait_ge(p_yb, j - 1)
                o = bank[5 + s][:, 0:D]
                for c in range(HC):
                    lhs = hThi[:, s, c * P:(c + 1) * P]
                    at = ds(e * (HC * D) + c * D, D)
                    pe.matmul(o, lhs, w2hi[:, at], start=c == 0, stop=False)
                    pe.matmul(o, lhs, w2lo[:, at], start=False, stop=False)
                pe.wait_ge(p_hlo, j + 1)
                for c in range(HC):
                    at = ds(e * (HC * D) + c * D, D)
                    ins = pe.matmul(o, hTlo[:, s, c * P:(c + 1) * P], w2hi[:, at], start=False, stop=c == HC - 1)
                ins.then_inc(p_y, 1)

            def expert(j):
                return pe.value_load(ti[0:1, 0, ds(j, 1)], min_val=0, max_val=E - 1)

            turn_x(0, 0)
            first_product(0, 0, expert(0))
            turn_x(1, 1)
            first_product(1, 1, expert(1))
            turn_x(2, 0)

            def round_(j, s):
                e = expert(j + 2)
                turn_h(j, s)
                first_product(j + 2, s, e)
                if not (isinstance(j, int) and j + 3 >= TILES):
                    turn_x(j + 3, 1 - s)
                e = expert(j)
                second_product(j, s, e)

            round_(0, 0)
            round_(1, 1)
            with pe.Fori(1, TILES // 2 - 2) as k:
                round_(2 * k, 0)
                round_(2 * k + 1, 1)
            round_(TILES - 4, 0)
            round_(TILES - 3, 1)
            for j in (TILES - 2, TILES - 1):
                e = expert(j)
                turn_h(j, j % 2)
                second_product(j, j % 2, e)


def kernel(x, src, dst, L0_gnn_weight, L0_gnn_attn_l, L0_gnn_attn_r, L0_ffn_gate_w, L0_ffn_gate_b, L0_ffn_W1,
           L0_ffn_b1, L0_ffn_W2, L0_ffn_b2):
    import numpy as np
    import concourse.bacc as bacc
    from concourse.bass_utils import run_bass_kernel_spmd

    x = np.asarray(x)
    n = x.shape[0]
    pad = padded_nodes(n) - n
    experts = np.shape(L0_ffn_gate_w)[1]

    def by_tile(index):
        a = np.pad(np.asarray(index)[:n], (0, pad)).reshape(-1, P, GT)
        return a.transpose(1, 0, 2)

    arrays = {
        "x": np.pad(x, ((0, pad), (0, 0))),
        "edges": np.ascontiguousarray(np.concatenate([by_tile(dst), by_tile(src)], axis=2)),
        "gnn_weight": np.ascontiguousarray(L0_gnn_weight),
        "attn_l": np.ascontiguousarray(L0_gnn_attn_l),
        "attn_r": np.ascontiguousarray(L0_gnn_attn_r),
        "gate_w": np.ascontiguousarray(L0_ffn_gate_w),
        "gate_b": np.ascontiguousarray(L0_ffn_gate_b),
        "w1": np.ascontiguousarray(L0_ffn_W1),
        "b1": np.ascontiguousarray(L0_ffn_b1),
        "w2": np.ascontiguousarray(L0_ffn_W2),
        "b2": np.ascontiguousarray(L0_ffn_b2),
    }
    nc = bacc.Bacc("TRN2", target_bir_lowering=False, num_devices=1)
    args = [nc.dram_tensor(k, a.shape, mybir.dt.from_np(a.dtype), kind="ExternalInput").ap()
            for k, a in arrays.items()]
    rows = n + pad + P * (1 + pieces(n, experts)[1])
    out = nc.dram_tensor("out", (rows, x.shape[1]), F32, kind="ExternalOutput").ap()
    gnn_moe(nc, n, *args, out)
    result = run_bass_kernel_spmd(nc, [arrays], core_ids=[0])
    return result.results[0]["out"][:n]
```

```python
from contextlib import ExitStack

import concourse.bass as bass
from concourse import mybir

F32 = mybir.dt.float32
F32R = mybir.dt.float32r
BF16 = mybir.dt.bfloat16
I32 = mybir.dt.int32
U32 = mybir.dt.uint32
ALU = mybir.AluOpType
ACT = mybir.ActivationFunctionType
AX = mybir.AxisListType
ds = bass.ds

P = 128
TOP = 2
GT = 7
EPS = 1e-5
SLOPE = 0.01
A_STEPS = 17
B_STEPS = 34
GUESS = float(0x5F3759DF)
AHEAD = 3
XR = 4
RING = 4
N_FOLD = 4
FAR = 1.0e6


def padded_nodes(n):
    return -(-n // (P * GT)) * P * GT


def pieces(n, experts):
    most = (TOP * n + experts * (P - 1)) // P
    return most, most - -(-TOP * n // P)


def back(i, ring=RING):
    return ring if i >= ring else i + GT - max(k for k in range(GT) if k % ring == i)


class Steps:

    def __init__(self, engine, sem, per_group=0):
        self.engine, self.sem, self.per = engine, sem, per_group
        self.base, self.n = 0, 0

    def begin(self, g):
        self.base, self.n = g * self.per, 0

    def end(self):
        assert self.n == self.per, (self.n, self.per)

    def did(self, ins):
        ins.then_inc(self.sem, 1)
        self.n += 1

    def wait(self):
        self.engine.wait_ge(self.sem, self.base + self.n)


def gnn_moe(nc, n, x, edges, gw, attn_l, attn_r, gate_w, gate_b, w1, b1, w2, b2, out):
    D = x.shape[1]
    H, DH = attn_l.shape
    E = gate_w.shape[1]
    HID = w1.shape[2]
    KC = D // P
    HC = HID // P
    NP = padded_nodes(n)
    GROUPS = NP // (P * GT)
    TILES, DUMMIES = pieces(n, E)
    ROW = D + 1 + E
    TOK, CW = D, D + 1
    CAP = NP + P
    XS_ROWS = E * CAP + DUMMIES * P
    assert GROUPS % 2 == 1 and GROUPS >= 5
    assert E == GROUPS + 1
    ZEROS = 16 * (-(-DUMMIES // GT) - (-(1 + DUMMIES) // GT))
    assert out.shape[0] == NP + P * (1 + DUMMIES)

    WIDTH = KC * HID
    assert WIDTH == HC * D
    XW = D + H
    xs = nc.dram_tensor("dispatched_rows", [XS_ROWS, ROW], F32).ap()
    table = nc.dram_tensor("transformed_rows", [NP, XW], F32).ap()
    src_scores = nc.dram_tensor("src_scores", [NP, H], F32).ap()

    with ExitStack() as ctx:
        def sb(name, shape, dt=F32):
            return ctx.enter_context(nc.sbuf_tensor(name, shape, dt))

        def sem(name):
            return ctx.enter_context(nc.semaphore(name))

        bank = [ctx.enter_context(nc.psum_tensor(f"bank{i}", [P, 512], F32)) for i in range(8)]

        w1hi = sb("w1hi", [P, E * KC * HID], F32R)
        w1lo = sb("w1lo", [P, E * KC * HID], F32R)
        w2hi = sb("w2hi", [P, E * HC * D], F32R)
        w2lo = sb("w2lo", [P, E * HC * D], F32R)
        w1s = sb("w1_stage", [P, KC * HID])
        w2s = sb("w2_stage", [P, HC * D])
        ident = sb("ident", [P, P])
        upper = sb("upper", [P, P], BF16)
        ones = sb("ones", [P, P], BF16)
        tokid = sb("tokid", [P, NP // P], I32)
        far = sb("far", [P, NP // P])
        keep = sb("keep", [P, NP // P])
        iota_e = sb("iota_e", [P, E])
        region0 = sb("region0", [P, E])
        ones32 = sb("ones32", [P, P])
        one8 = sb("one8", [P, E])
        iota_j = sb("iota_j", [1, TILES])
        padrow = sb("padrow", [P, ROW])
        wcat = sb("wcat", [P, KC, D + 2 * H])
        gatew = sb("gatew", [P, KC, E])
        gateb = sb("gateb", [P, E])
        edge = sb("edge", [P, GROUPS, 2 * GT], I32)
        edge_g = sb("edge_g", [P, 2, 2 * GT], I32)
        turned = sb("turned", [P, RING, D])
        NODES, XTS = GT * D, GT * (D + 2 * H)
        shared = sb("shared", [P, max(2 * NODES + 2 * XTS, NODES + 2 * GT * XW + GT * ROW,
                                      2 * HID + E * (D + HID))])
        xa = [shared[:, k * NODES:(k + 1) * NODES].rearrange("p (t d) -> p t d", t=GT) for k in range(2)]
        xt = [shared[:, 2 * NODES + k * XTS:2 * NODES + (k + 1) * XTS].rearrange("p (t d) -> p t d", t=GT)
              for k in range(2)]
        al = sb("al", [P, GROUPS, GT * H])
        xg = xa[0]
        gx = [shared[:, NODES + k * GT * XW:NODES + (k + 1) * GT * XW].rearrange("p (t d) -> p t d", t=GT)
              for k in range(2)]
        a_scale = sb("a_scale", [P, 2, GT])
        gal = sb("gal", [P, 2, GT, H])
        attnl, attnr = turned[:, 0, :], turned[:, 1, :]
        rows = sb("rows", [P, GT, ROW])
        R1 = NODES + 2 * GT * XW
        out_rows = [rows, shared[:, R1:R1 + GT * ROW].rearrange("p (t d) -> p t d", t=GT)]
        st = sb("st", [P, GT, 6])
        ln = [sb(f"ln_{i}", [P, GT]) for i in range(10)]
        sc = sb("sc", [P, GT, H])
        lr = sb("lr", [P, GT, H])
        hm = sb("hm", [P, GT])
        he = sb("he", [P, GT, H])
        hsum = sb("hsum", [P, GT])
        hrec = sb("hrec", [P, GT])
        alpha = sb("alpha", [P, GT, H])
        prod = sb("prod", [P, 2, D])
        msg = sb("msg", [P, RING, DH])
        raw = sb("raw", [P, GT, E])
        lg = sb("lg", [P, GT, E])
        mx = sb("mx", [P, GT, 8])
        mi = sb("mi", [P, GT, 8], U32)
        mif = sb("mif", [P, GT, TOP])
        em = sb("em", [P, GT, E])
        ex = sb("ex", [P, GT, E])
        esum = sb("esum", [P, GT])
        erec = sb("erec", [P, GT])
        pr = sb("pr", [P, GT, E])
        mask = sb("mask", [P, GT, TOP, E])
        both = sb("both", [P, GT, E])
        both16 = sb("both16", [P, GT, E], BF16)
        rank = sb("rank", [P, GT, E])
        mrank = sb("mrank", [P, GT, TOP, E])
        posf = sb("posf", [P, GT, TOP])
        posi = sb("posi", [P, 2, GT, TOP], I32)
        filled = sb("filled", [P, E])
        filled_i = sb("filled_i", [1, E], I32)
        cnt = sb("cnt", [1, E])
        cnt_i = sb("cnt_i", [1, E], I32)
        nt_i = sb("nt_i", [1, E], I32)
        nt = sb("nt", [1, E])
        upto = sb("upto", [1, E])
        TE = TILES * E
        ge = w1s[0:1, 0:TE].rearrange("p (j e) -> p j e", e=E)
        gn = w2s[0:1, 0:TE].rearrange("p (j e) -> p j e", e=E)
        tf = prod[0:1, :, :].rearrange("p s d -> p (s d)")[:, 0:4 * TILES].rearrange("p (k j) -> p k j", k=4)
        ti = sb("ti", [1, 4, TILES], I32)
        hb = shared[:, 0:2 * HID].rearrange("p (s m) -> p s m", s=2)
        b2bc = shared[:, 2 * HID:2 * HID + E * D]
        b1bc = shared[:, 2 * HID + E * D:2 * HID + E * (D + HID)]
        yb = prod
        xin = rows
        xin_flat = rows[:, :, :].rearrange("p s m -> p (s m)")
        xThi = sb("xThi", [P, 2, KC * P], F32R)
        xTlo = sb("xTlo", [P, 2, KC * P], F32R)
        hThi = sb("hThi", [P, 2, HID], F32R)
        hTlo = sb("hTlo", [P, 2, HID], F32R)
        cwring = sb("cwring", [P, TILES])
        toknow = sb("toknow", [P, XR], I32)

        s_edge, s_const, s_vw, s_bias = sem("s_edge"), sem("s_const"), sem("s_vw"), sem("s_bias")
        s_w, s_whi, s_wlo = sem("s_w"), sem("s_whi"), sem("s_wlo")
        s_pool, s_zero, s_fold = sem("s_pool"), sem("s_zero"), sem("s_fold")
        s_settled, s_sp_settled = sem("s_settled"), sem("s_sp_settled")
        a_in, a_store = [sem(f"a_in{i}") for i in range(2)], [sem(f"a_store{i}") for i in range(2)]
        a_rstd, a_turn, a_turned, a_xt, a_out, a_al, a_steps, a_alstore = (
            sem(k) for k in ("a_rstd", "a_turn", "a_turned", "a_xt", "a_out", "a_al", "a_steps", "a_alstore"))
        s_sums, s_centred = sem("s_sums"), sem("s_centred")
        s_gath = [[sem(f"s_gath{s}_{i}") for i in range(GT)] for s in range(2)]
        s_scat = [[sem(f"s_scat{s}_{i}") for i in range(GT)] for s in range(2)]
        s_edge_g, s_steps, s_b1 = sem("s_edge_g"), sem("s_steps"), sem("s_b1")
        s_harg, s_hexp, s_alpha = sem("s_harg"), sem("s_hexp"), sem("s_alpha")
        s_prod, s_msg, s_x2, s_rstd = sem("s_prod"), sem("s_msg"), sem("s_x2"), sem("s_rstd")
        s_nr, s_t2, s_e2, s_gate = sem("s_nr"), sem("s_t2"), sem("s_e2"), sem("s_gate")
        s_garg, s_gexp, s_both, s_ranks = sem("s_garg"), sem("s_gexp"), sem("s_both"), sem("s_ranks")
        s_pos, s_cw = sem("s_pos"), sem("s_cw")
        s_xin, s_out = sem("s_xin"), sem("s_out")
        s_tab, s_tables, s_pads = sem("s_tab"), sem("s_tables"), sem("s_pads")
        p_xin = [sem(f"p_xin{i}") for i in range(XR)]
        p_add = [sem(f"p_add{i}") for i in range(2)]
        p_xT, p_xhi, p_xlo, p_h, p_bias, p_gelu, p_hT, p_hhi, p_hlo, p_y, p_yb, p_yout, p_cw, p_tok = (
            sem(k) for k in ("p_xT", "p_xhi", "p_xlo", "p_h", "p_bias", "p_gelu", "p_hT", "p_hhi", "p_hlo", "p_y",
                             "p_yb", "p_yout", "p_cw", "p_tok"))

        block = ctx.enter_context(nc.Block())
        LAST = GROUPS - 1

        def tile_rows(dram, g):
            r = g * (GT * P)
            part = dram[r:r + GT * P, :] if isinstance(g, int) else dram[ds(r, GT * P), :]
            return part.rearrange("(p t) c -> p t c", p=P)

        def node_groups(engine, body):
            body(0, 0, 0)
            body(1, 1, 0)
            with engine.Fori(1, GROUPS // 2) as k:
                body(2 * k, 0, k)
                body(2 * k + 1, 1, k)
            body(LAST, 0, LAST // 2)

        def slot_used(g, i, ring=RING):
            return not (isinstance(g, int) and g == 0 and i < ring)

        @block.sync
        def _(sp):
            sp.dma_start(edge[:, :, :], edges).then_inc(s_edge, 16)

            def load_x(g):
                sp.dma_start(xg[:, :, :], tile_rows(x, g)).then_inc(s_xin, 16)

            def load_expert(e):
                a = w1[e:e + 1] if isinstance(e, int) else w1[ds(e, 1)]
                b = w2[e:e + 1] if isinstance(e, int) else w2[ds(e, 1)]
                sp.dma_start(w1s[:, :].rearrange("p (c m) -> p c m", c=KC),
                             a.rearrange("e (c p) m -> p (e c) m", p=P)).then_inc(s_w, 16)
                sp.dma_start(w2s[:, :].rearrange("p (c m) -> p c m", c=HC),
                             b.rearrange("e (c p) m -> p (e c) m", p=P)).then_inc(s_w, 16)

            sp.dma_start(wcat[:, :, 0:D], gw.rearrange("(c p) m -> p c m", p=P)).then_inc(s_vw, 16)
            sp.dma_start(attnl[:, :], attn_l.rearrange("h d -> (h d)").partition_broadcast(P)).then_inc(s_vw, 16)
            sp.dma_start(attnr[:, :], attn_r.rearrange("h d -> (h d)").partition_broadcast(P)).then_inc(s_vw, 16)
            sp.dma_start(xa[0], tile_rows(x, 0)).then_inc(a_in[0], 16)
            sp.dma_start(gatew[:, :, :], gate_w.rearrange("(c p) m -> p c m", p=P)).then_inc(s_bias, 16)
            sp.dma_start(gateb[:, :], gate_b.partition_broadcast(P)).then_inc(s_bias, 16)
            sp.dma_start(xa[1], tile_rows(x, 1)).then_inc(a_in[1], 16)

            def settle():
                sp.sem_inc(s_sp_settled, 1)

            def a_group(g, s, h):
                if not (isinstance(g, int) and g + 2 >= GROUPS):
                    sp.wait_ge(a_turn, GT * (g + 1))
                    settle()
                    sp.wait_ge(a_rstd, g + 1)
                    sp.dma_start(xa[s], tile_rows(x, g + 2)).then_inc(a_in[s], 16)
                sp.wait_ge(a_out, GT * (g + 1))
                sp.dma_start(tile_rows(table, g), xt[s][:, :, 0:XW]).then_inc(a_store[s], 16)

            a_group(0, 0, 0)
            a_group(1, 1, 0)
            load_expert(0)
            with sp.Fori(1, GROUPS // 2 - 1) as k:
                a_group(2 * k, 0, k)
                a_group(2 * k + 1, 1, k)
            for g in range(GROUPS - GROUPS % 2 - 2, GROUPS):
                a_group(g, g % 2, g // 2)
            sp.wait_ge(a_al, GROUPS)
            sp.dma_start(src_scores.rearrange("(g p t) h -> p g (t h)", g=GROUPS, p=P), al[:, :, :]
                         ).then_inc(a_alstore, 16)
            load_x(0)

            def group(g, last):
                sp.wait_ge(s_wlo, 2 * (g + 1))
                load_expert(g + 1)
                sp.wait_ge(s_x2, GT * (g + 1))
                sp.dma_start(tile_rows(out, g), xg[:, :, :]).then_inc(s_out, 16)
                if not last:
                    sp.wait_ge(s_out, 16 * (g + 1))
                    settle()
                    sp.wait_ge(s_nr, GT * (g + 1))
                    sp.wait_ge(s_t2, GT * (g + 1))
                    load_x(g + 1)

            group(0, False)
            with sp.Fori(1, LAST) as g:
                group(g, False)
            group(LAST, True)

            sp.wait_ge(s_prod, GT * GROUPS)
            for i in range(GT):
                sp.wait_ge(s_scat[1][i], 32 * (GROUPS // 2))
            sp.dma_start(b1bc, b1.rearrange("e m -> (e m)").partition_broadcast(P)).then_inc(s_b1, 16)
            sp.wait_ge(s_out, 16 * GROUPS)
            sp.wait_ge(s_nr, GT * GROUPS)
            sp.wait_ge(s_t2, GT * GROUPS)
            sp.dma_start(b2bc, b2.rearrange("e m -> (e m)").partition_broadcast(P)).then_inc(s_b1, 16)
            sp.wait_ge(s_tables, 1)
            sp.wait_ge(s_pool, 1)
            for e in range(E):
                r = sp.value_load(filled_i[0:1, e:e + 1], min_val=e * CAP, max_val=e * CAP + NP)
                sp.dma_start(xs[ds(r, P), :], padrow[:, :]).then_inc(s_pads, 16)
            sp.wait_ge(s_pads, 16 * E)
            sp.wait_ge(s_zero, ZEROS)
            for i in range(GT):
                sp.wait_ge(s_scat[0][i], 32 * ((GROUPS + 1) // 2))

            def load_tile(j, s):
                if not (isinstance(j, int) and j < XR):
                    sp.wait_ge(p_xT, j - XR + 1)
                    sp.wait_ge(p_cw, j - XR + 1)
                    sp.wait_ge(p_tok, j - XR + 1)
                r = sp.value_load(ti[0:1, 1, ds(j, 1)], min_val=0, max_val=XS_ROWS - P)
                sp.dma_start(xin[:, s, :], xs[ds(r, P), :]).then_inc(p_xin[s], 16)

            for j in range(XR):
                load_tile(j, j)
            with sp.Fori(1, TILES // XR) as k:
                for i in range(XR):
                    load_tile(XR * k + i, i)
            for j in range(TILES - TILES % XR, TILES):
                load_tile(j, j % XR)

        @block.gpsimd
        def _(pool):
            pool.memset(rows[:, :, :], 0.0).then_inc(s_const, 1)
            pool.memset(padrow[:, :], 0.0).then_inc(s_const, 1)
            pool.memset(ident[:, :], 0.0).then_inc(s_const, 1)
            pool.memset(upper[:, :], 1.0).then_inc(s_const, 1)
            pool.memset(ones[:, :], 1.0).then_inc(s_const, 1)
            pool.memset(ones32[:, :], 1.0).then_inc(s_const, 1)
            pool.memset(one8[:, :], 1.0).then_inc(s_const, 1)
            pool.iota(tokid[:, :], [[P * GT, GROUPS], [1, GT]], base=0, channel_multiplier=GT).then_inc(s_const, 1)
            pool.memset(keep[:, :], 1.0).then_inc(s_const, 1)
            pool.memset(far[:, :], 0.0).then_inc(s_const, 1)
            pool.iota(iota_e[:, :], [[1, E]], base=0, channel_multiplier=0,
                      allow_small_or_imprecise_dtypes=True).then_inc(s_const, 1)
            pool.iota(region0[:, :], [[CAP, E]], base=0, channel_multiplier=0,
                      allow_small_or_imprecise_dtypes=True).then_inc(s_const, 1)
            pool.iota(filled[:, :], [[CAP, E]], base=0, channel_multiplier=0,
                      allow_small_or_imprecise_dtypes=True).then_inc(s_const, 1)
            pool.iota(iota_j[:, :], [[1, TILES]], base=0, channel_multiplier=0,
                      allow_small_or_imprecise_dtypes=True).then_inc(s_const, 1)
            pool.wait_ge(s_const, 14)
            pool.affine_select(ident[:, :], ident[:, :], [[1, P]], ALU.not_equal, 1.0, base=0,
                               channel_multiplier=-1).then_inc(s_const, 1)
            pool.affine_select(upper[:, :], upper[:, :], [[1, P]], ALU.is_gt, 0.0, base=0,
                               channel_multiplier=-1).then_inc(s_const, 1)
            pool.affine_select(keep[:, :], keep[:, :], [[-P * GT, GROUPS], [-1, GT]], ALU.is_gt, 0.0, base=n,
                               channel_multiplier=-GT).then_inc(s_const, 1)
            pool.affine_select(far[:, :], far[:, :], [[-P * GT, GROUPS], [-1, GT]], ALU.is_gt, FAR, base=n,
                               channel_multiplier=-GT).then_inc(s_const, 1)
            pool.iota(rows[:, :, TOK:TOK + 1].bitcast(I32), [[P, GT], [1, 1]], base=NP,
                      channel_multiplier=1).then_inc(s_const, 1)
            pool.iota(padrow[:, TOK:TOK + 1].bitcast(I32), [[1, 1]], base=NP, channel_multiplier=1).then_inc(s_pool, 1)
            pool.wait_ge(s_edge, 16)

            def settle():
                pool.sem_inc(s_settled, 1)

            def gathers(g, s):
                if not isinstance(g, int) or g > 1:
                    pool.wait_ge(s_prod, GT * (g - 1))
                    settle()
                at = edge[:, g, :] if isinstance(g, int) else edge[:, ds(g, 1), :].rearrange("p a t -> p (a t)")
                pool.tensor_copy(edge_g[:, s, :], at).then_inc(s_edge_g, 1)
                pool.wait_ge(s_edge_g, g + 1)
                settle()
                for i in range(GT):
                    pool.indirect_dma_start(gx[s][:, i, :], None, table,
                                            bass.IndirectOffsetOnAxis(edge_g[:, s, i:i + 1], 0)
                                            ).then_inc(s_gath[s][i], 16)
                    pool.indirect_dma_start(gal[:, s, i, :], None, src_scores,
                                            bass.IndirectOffsetOnAxis(edge_g[:, s, GT + i:GT + i + 1], 0)
                                            ).then_inc(s_gath[s][i], 16)

            def scatters(g, s):
                pool.wait_ge(s_nr, GT * (g + 1))
                settle()
                pool.wait_ge(s_pos, g + 1)
                settle()
                for i in range(GT):
                    for k in range(TOP):
                        pool.indirect_dma_start(xs, bass.IndirectOffsetOnAxis(posi[:, s, i, k:k + 1], 0),
                                                out_rows[s][:, i, :], None, bounds_check=XS_ROWS - 1, oob_is_err=False
                                                ).then_inc(s_scat[s][i], 16)

            pool.wait_ge(s_const, 19)
            for t0 in range(0, DUMMIES, GT):
                m = min(GT, DUMMIES - t0)
                pool.dma_start(xs[E * CAP + t0 * P:E * CAP + (t0 + m) * P, :].rearrange("(t p) c -> p t c", p=P),
                               rows[:, 0:m, :]).then_inc(s_zero, 16)
            for t0 in range(0, 1 + DUMMIES, GT):
                m = min(GT, 1 + DUMMIES - t0)
                pool.dma_start(out[NP + t0 * P:NP + (t0 + m) * P, :].rearrange("(t p) c -> p t c", p=P),
                               rows[:, 0:m, 0:D]).then_inc(s_zero, 16)
            def set_apart(g, s, h):
                pool.wait_ge(a_out, GT * (g + 1))
                pool.tensor_copy(al[:, g, :].rearrange("p (t h) -> p t h", t=GT) if isinstance(g, int)
                                 else al[:, ds(g, 1), :].rearrange("p a (t h) -> p (a t) h", t=GT),
                                 xt[s][:, :, XW:XW + H]).then_inc(a_al, 1)

            node_groups(pool, set_apart)
            for s in range(2):
                pool.wait_ge(a_store[s], 16 * ((GROUPS + 1 - s) // 2))
            pool.wait_ge(a_alstore, 16)
            for g in range(3):
                gathers(g, g % 2)
            with pool.Fori(0, (GROUPS - 3) // 2) as k:
                scatters(2 * k, 0)
                gathers(2 * k + 3, 1)
                scatters(2 * k + 1, 1)
                gathers(2 * k + 4, 0)
            for g in range(GROUPS - 3, GROUPS):
                scatters(g, g % 2)

            pool.wait_ge(s_tables, 1)
            pool.wait_ge(s_out, 16 * GROUPS)
            pool.wait_ge(s_zero, ZEROS)

            def half(j):
                return j // 2 if isinstance(j, int) else j >> 1

            def keep_tokens(j, i):
                n_load = j // XR + 1 if isinstance(j, int) else (j >> 2) + 1
                pool.wait_ge(p_xin[i], 16 * n_load)
                settle()
                pool.tensor_copy(toknow[:, i:i + 1], xin[:, i, TOK:TOK + 1].bitcast(I32)).then_inc(p_tok, 1)

            def add_tile(j, i, ahead=True):
                s = i % 2
                first = isinstance(j, int) and j < 2
                if not first:
                    pool.wait_ge(p_add[s], 16 * half(j))
                if ahead:
                    keep_tokens(j + 2, (i + 2) % XR)
                settle()
                before = pool.value_load(ti[0:1, 2, ds(j, 1)], min_val=2, max_val=TILES)
                if not (first and j == 0):
                    pool.wait_ge(p_add[0], 16 * ((before + 1) >> 1))
                    settle()
                if not first:
                    pool.wait_ge(p_add[1], 16 * (before >> 1))
                    settle()
                pool.wait_ge(p_tok, j + 1)
                pool.wait_ge(p_yout, j + 1)
                settle()
                pool.indirect_dma_start(out, bass.IndirectOffsetOnAxis(toknow[:, i:i + 1], 0), yb[:, s, :], None,
                                        compute_op=ALU.add).then_inc(p_add[s], 16)

            keep_tokens(0, 0)
            keep_tokens(1, 1)
            for j in range(XR):
                add_tile(j, j)
            with pool.Fori(1, (TILES - 2) // XR) as k:
                for i in range(XR):
                    add_tile(XR * k + i, i)
            for j in range(XR * ((TILES - 2) // XR), TILES):
                add_tile(j, j % XR, j + 2 < TILES)
            for s in range(2):
                pool.wait_ge(p_add[s], 16 * ((TILES + 1 - s) // 2))

        @block.scalar
        def _(act):
            def split_high(e):
                act.wait_ge(s_w, 32 * (e + 1))
                act.activation(w1hi[:, ds(e * (KC * HID), KC * HID)], w1s[:, :], ACT.Copy).then_inc(s_whi, 1)
                act.activation(w2hi[:, ds(e * (HC * D), HC * D)], w2s[:, :], ACT.Copy).then_inc(s_whi, 1)

            def product_out(g, s, i):
                act.wait_ge(a_xt, GT * g + i + 1)
                if i == 0:
                    act.wait_ge(a_rstd, g + 1)
                act.activation(xt[s][:, i, :], bank[RING + i % RING][:, 0:D + 2 * H], ACT.Copy,
                               scale=a_scale[:, s, i:i + 1]).then_inc(a_out, 1)

            def a_group(g, s, h):
                for i in range(GT):
                    n_tile = GT * g + i + 1
                    act.wait_ge(a_turn, n_tile)
                    if slot_used(g, i):
                        act.wait_ge(a_xt, n_tile - back(i))
                    act.activation(turned[:, i % RING, :], bank[i % RING][:, 0:D], ACT.Copy).then_inc(a_turned, 1)
                    if i == 1 and not (isinstance(g, int) and g < 2):
                        act.wait_ge(a_store[s], 16 * h)
                        act.wait_ge(a_al, g - 1)
                    if i:
                        product_out(g, s, i - 1)
                    elif not isinstance(g, int) or g > 0:
                        product_out(g - 1, 1 - s, GT - 1)

            node_groups(act, a_group)
            product_out(LAST, LAST % 2, GT - 1)
            split_high(0)

            def group(g, s, h):
                act.wait_ge(s_harg, g + 1)
                act.activation(he[:, :, :], he[:, :, :], ACT.Exp).then_inc(s_hexp, 1)
                act.wait_ge(s_alpha, g + 1)

                def weigh_heads(i):
                    if slot_used(g, i, 2):
                        act.wait_ge(s_msg, GT * g + i + 1 - back(i, 2))
                    for k in range(H):
                        at = slice(k * DH, (k + 1) * DH)
                        ins = act.activation(prod[:, i % 2, at], gx[s][:, i, at], ACT.Copy, scale=alpha[:, i, k:k + 1])
                    ins.then_inc(s_prod, 1)

                def turned_out(i):
                    act.wait_ge(s_t2, GT * g + i + 1)
                    if slot_used(g, i):
                        act.wait_ge(s_gate, GT * g + i + 1 - back(i))
                    act.activation(turned[:, i % RING, :], bank[i % RING][:, 0:D], ACT.Copy).then_inc(s_e2, 1)

                LAG = 3
                for i in range(GT + LAG):
                    if i < GT:
                        weigh_heads(i)
                    if i >= LAG:
                        turned_out(i - LAG)
                split_high(g + 1)
                act.wait_ge(s_rstd, g + 1)
                if isinstance(g, int) and g == 0:
                    act.wait_ge(s_zero, ZEROS)
                for i in range(GT):
                    if not isinstance(g, int) or g > 1:
                        act.wait_ge(s_scat[s][i], 32 * h)
                    act.activation(out_rows[s][:, i, 0:D], xg[:, i, :], ACT.Identity, bias=ln[8][:, i:i + 1],
                                   scale=ln[6][:, i:i + 1]).then_inc(s_nr, 1)
                act.wait_ge(s_garg, g + 1)
                act.activation(ex[:, :, :], em[:, :, :], ACT.Exp).then_inc(s_gexp, 1)

            node_groups(act, group)

            def half(j):
                return j // 2 if isinstance(j, int) else j >> 1

            def x_high(j, s):
                act.wait_ge(p_xT, j + 1)
                if not isinstance(j, int) or j >= 2:
                    act.wait_ge(p_h, j - 1)
                act.activation(xThi[:, s, :], bank[0][:, 0:D], ACT.Copy).then_inc(p_xhi, 1)

            def gelu(j, s):
                act.wait_ge(p_bias, j + 1)
                act.activation(hb[:, s, :], hb[:, s, :], ACT.Gelu).then_inc(p_gelu, 1)

            def h_high(j, s):
                act.wait_ge(p_hT, j + 1)
                if not isinstance(j, int) or j >= 2:
                    act.wait_ge(p_y, j - 1)
                act.activation(hThi[:, s, :], bank[3 + s][:, :], ACT.Copy).then_inc(p_hhi, 1)

            def y_out(j, s):
                act.wait_ge(p_yb, j + 1)
                act.activation(yb[:, s, :], yb[:, s, :], ACT.Copy, scale=cwring[:, ds(j, 1)]).then_inc(p_yout, 1)

            x_high(0, 0)
            gelu(0, 0)
            x_high(1, 1)

            def step(j, s):
                if not (isinstance(j, int) and j + 1 >= TILES):
                    x_high(j + 1, 1 - s)
                gelu(j, s)
                h_high(j - 1, 1 - s)
                if not isinstance(j, int) or j >= 2:
                    y_out(j - 2, s)

            step(1, 1)
            step(2, 0)
            step(3, 1)
            with act.Fori(2, (TILES - 1) // 2) as k:
                step(2 * k, 0)
                step(2 * k + 1, 1)
            for j in range((TILES - 1) // 2 * 2, TILES):
                step(j, j % 2)
            y_out(TILES - 2, TILES % 2)
            h_high(TILES - 1, 1 - TILES % 2)
            y_out(TILES - 1, 1 - TILES % 2)

        @block.vector
        def _(dve):
            def split_low(e, which):
                at = ds(e * (KC * HID), KC * HID)
                hi, lo, stage = ((w1hi, w1lo, w1s), (w2hi, w2lo, w2s))[which]
                dve.wait_ge(s_whi, 2 * e + 1 + which)
                dve.tensor_tensor(lo[:, at], stage[:, :], hi[:, at].bitcast(F32), ALU.subtract).then_inc(s_wlo, 1)

            dve.wait_ge(s_vw, 48)
            fold = Steps(dve, s_fold)
            for a, at in ((attnr, D), (attnl, D + H)):
                fold.did(dve.tensor_tensor(prod[:, 0:KC, :], wcat[:, :, 0:D],
                                           a.unsqueeze(1).to_broadcast([P, KC, D]), ALU.mult))
                fold.wait()
                fold.did(dve.tensor_reduce(wcat[:, :, at:at + H],
                                           prod[:, 0:KC, :].rearrange("p c (h d) -> p c h d", h=H), AX.X, ALU.add))
                fold.wait()
            FOLDS = fold.n
            assert FOLDS == N_FOLD
            dve.wait_ge(s_const, 19)

            def centre():
                dve.wait_ge(s_sums, 1)
                for c in range(KC):
                    dve.scalar_tensor_tensor(wcat[:, c, :], bank[7][:, 0:D + 2 * H], -1.0 / D, wcat[:, c, :], ALU.mult,
                                             ALU.add).then_inc(s_centred, 1)
                    dve.scalar_tensor_tensor(gatew[:, c, :], bank[6][:, 0:E], -1.0 / D, gatew[:, c, :], ALU.mult,
                                             ALU.add).then_inc(s_centred, 1)

            def variance(t):
                msum, md, vs, mean, md2, vs2, veps = (ln[k][:, :] for k in (0, 1, 2, 3, 4, 9, 5))
                dve.tensor_tensor(vs, st[:, :, 2], st[:, :, 5], ALU.add)
                t.did(dve.tensor_tensor(md, st[:, :, 1], st[:, :, 4], ALU.subtract))
                dve.tensor_tensor(msum, st[:, :, 1], st[:, :, 4], ALU.add)
                t.wait()
                t.did(dve.tensor_tensor(md2, md, md, ALU.mult))
                t.did(dve.tensor_scalar(vs2, vs, 1.0 / D, EPS, ALU.mult, ALU.add))
                t.wait()
                t.did(dve.scalar_tensor_tensor(veps, md2, 0.25, vs2, ALU.mult, ALU.add))
                t.did(dve.tensor_scalar(mean, msum, 0.5, None, ALU.mult))
                t.wait()

            def rstd(t, result, free=None):
                minus_half, square, part_, veps, guess, r = (ln[k] for k in (1, 2, 4, 5, 6, 7))
                t.did(dve.tensor_scalar(guess[:, :].bitcast(I32), veps[:, :].bitcast(I32), 1, None,
                                        ALU.logical_shift_right))
                dve.tensor_scalar(minus_half[:, :], veps[:, :], -0.5, None, ALU.mult)
                t.wait()
                t.did(dve.tensor_scalar(r[:, :].bitcast(I32), guess[:, :].bitcast(I32), -1.0, GUESS, ALU.mult, ALU.add))
                t.wait()
                for step in range(3):
                    y, refined = (r[:, :], guess[:, :]) if step % 2 == 0 else (guess[:, :], r[:, :])
                    if step == 2:
                        refined = result
                        if free:
                            free()
                    t.did(dve.tensor_tensor(square[:, :], y, y, ALU.mult))
                    t.wait()
                    t.did(dve.tensor_tensor(part_[:, :], square[:, :], minus_half[:, :], ALU.mult))
                    t.wait()
                    t.did(dve.scalar_tensor_tensor(refined, part_[:, :], 1.5, y, ALU.add, ALU.mult))
                    t.wait()

            ta = Steps(dve, a_steps, A_STEPS)

            def a_group(g, s, h):
                dve.wait_ge(a_in[s], 16 * (h + 1))
                for i in range(GT):
                    ins = dve.bn_stats(st[:, i, :], xa[s][:, i, :])
                ta.begin(g)
                ta.did(ins)
                if isinstance(g, int) and g == 0:
                    centre()
                ta.wait()
                variance(ta)

                def free():
                    if not (isinstance(g, int) and g < 2):
                        dve.wait_ge(a_out, GT * (g - 1))

                rstd(ta, a_scale[:, s, :], free)
                dve.sem_inc(a_rstd, 1)
                ta.end()

            node_groups(dve, a_group)
            split_low(0, 0)
            split_low(0, 1)

            t = Steps(dve, s_steps, B_STEPS)

            def group(g, s, h):
                t.begin(g)
                for i in range(GT):
                    dve.wait_ge(s_gath[s][i], 32 * (h + 1))
                t.did(dve.tensor_tensor(sc[:, :, :], gx[s][:, :, D:XW], gal[:, s, :, :], ALU.add))
                t.wait()
                t.did(dve.scalar_tensor_tensor(lr[:, :, :], sc[:, :, :], SLOPE, sc[:, :, :], ALU.mult, ALU.max))
                t.wait()
                t.did(dve.tensor_reduce(hm[:, :], lr[:, :, :], AX.X, ALU.max))
                t.wait()
                dve.tensor_tensor(he[:, :, :], lr[:, :, :], hm[:, :].unsqueeze(2).to_broadcast([P, GT, H]),
                                  ALU.subtract).then_inc(s_harg, 1)
                dve.wait_ge(s_hexp, g + 1)
                t.did(dve.tensor_reduce(hsum[:, :], he[:, :, :], AX.X, ALU.add))
                t.wait()
                t.did(dve.reciprocal(hrec[:, :], hsum[:, :]))
                t.wait()
                dve.tensor_tensor(alpha[:, :, :], he[:, :, :], hrec[:, :].unsqueeze(2).to_broadcast([P, GT, H]),
                                  ALU.mult).then_inc(s_alpha, 1)
                dve.wait_ge(s_xin, 16 * (g + 1))

                def heads(i):
                    dve.wait_ge(s_prod, GT * g + i + 1)
                    dve.tensor_reduce(msg[:, i % RING, :], prod[:, i % 2, :].rearrange("p (h d) -> p d h", h=H),
                                      AX.X, ALU.add).then_inc(s_msg, 1)

                def residual(i):
                    dve.wait_ge(s_msg, GT * g + i + 1)
                    xv = xg[:, i, :].rearrange("p (h d) -> p h d", h=H)
                    dve.tensor_tensor(xv, xv, msg[:, i % RING, :].unsqueeze(1).to_broadcast([P, H, DH]), ALU.add
                                      ).then_inc(s_x2, 1)

                for i in range(GT + 2):
                    if i < GT:
                        heads(i)
                    if 1 <= i <= GT:
                        residual(i - 1)
                    if i >= 2:
                        dve.wait_ge(s_x2, GT * g + i - 1)
                        ins = dve.bn_stats(st[:, i - 2, :], xg[:, i - 2, :])
                t.did(ins)
                t.wait()
                variance(t)
                rstd(t, ln[6][:, :])
                dve.scalar_tensor_tensor(ln[8][:, :], ln[3][:, :], -1.0, ln[6][:, :], ALU.mult, ALU.mult
                                         ).then_inc(s_rstd, 1)
                at = ds(g * GT, GT)
                dve.wait_ge(s_gate, GT * (g + 1))
                t.did(dve.tensor_tensor(raw[:, :, :], bank[5][:, 0:GT * E].rearrange("p (t e) -> p t e", e=E),
                                        ln[6][:, :].unsqueeze(2).to_broadcast([P, GT, E]), ALU.mult))
                t.wait()
                t.did(dve.tensor_tensor(lg[:, :, :], raw[:, :, :],
                                        gateb[:, :].unsqueeze(1).to_broadcast([P, GT, E]), ALU.add))
                t.wait()
                split_low(g + 1, 0)
                for i in range(GT):
                    ins = dve.max(mx[:, i, :], lg[:, i, :])
                t.did(ins)
                t.wait()
                dve.tensor_tensor(em[:, :, :], lg[:, :, :], mx[:, :, 0:1].to_broadcast([P, GT, E]),
                                  ALU.subtract).then_inc(s_garg, 1)
                for i in range(GT):
                    ins = dve.max_index(mi[:, i, :], mx[:, i, :], lg[:, i, :])
                t.did(ins)
                t.wait()
                t.did(dve.tensor_copy(mif[:, :, :], mi[:, :, 0:TOP]))
                t.wait()
                t.did(dve.tensor_tensor(mask[:, :, :, :], mif[:, :, :].unsqueeze(3).to_broadcast([P, GT, TOP, E]),
                                        iota_e[:, :].unsqueeze(1).unsqueeze(1).to_broadcast([P, GT, TOP, E]),
                                        ALU.is_equal))
                t.wait()
                t.did(dve.tensor_tensor(both[:, :, :], mask[:, :, 0, :], mask[:, :, 1, :], ALU.add))
                t.wait()
                dve.tensor_tensor(both16[:, :, :], both[:, :, :], keep[:, at].unsqueeze(2).to_broadcast([P, GT, E]),
                                  ALU.mult).then_inc(s_both, 1)
                split_low(g + 1, 1)
                dve.wait_ge(s_gexp, g + 1)
                dve.tensor_tensor(pr[:, :, :], ex[:, :, :], both[:, :, :], ALU.mult)
                t.did(dve.tensor_reduce(esum[:, :], ex[:, :, :], AX.X, ALU.add))
                t.wait()
                t.did(dve.reciprocal(erec[:, :], esum[:, :]))
                t.wait()
                if isinstance(g, int) and g == 0:
                    dve.wait_ge(s_zero, ZEROS)
                if not isinstance(g, int) or g > 1:
                    for i in range(GT):
                        dve.wait_ge(s_scat[s][i], 32 * h)
                dve.tensor_copy(out_rows[s][:, 0:GT, TOK].bitcast(I32), tokid[:, at])
                dve.tensor_tensor(out_rows[s][:, 0:GT, CW:ROW], pr[:, :, :],
                                  erec[:, :].unsqueeze(2).to_broadcast([P, GT, E]), ALU.mult).then_inc(s_cw, 1)
                dve.wait_ge(s_ranks, g + 1)
                t.did(dve.tensor_tensor(rank[:, :, :], bank[6][:, 0:GT * E].rearrange("p (t e) -> p t e", e=E),
                                        filled[:, :].unsqueeze(1).to_broadcast([P, GT, E]), ALU.add))
                t.wait()
                dve.tensor_tensor(filled[:, :], bank[6][:, 64:64 + E], filled[:, :], ALU.add)
                t.did(dve.tensor_tensor(mrank[:, :, :, :], mask[:, :, :, :],
                                        rank[:, :, :].unsqueeze(2).to_broadcast([P, GT, TOP, E]), ALU.mult))
                t.wait()
                t.did(dve.tensor_reduce(posf[:, :, :], mrank[:, :, :, :], AX.X, ALU.add))
                t.wait()
                dve.tensor_tensor(posi[:, s, :, :], posf[:, :, :], far[:, at].unsqueeze(2).to_broadcast([P, GT, TOP]),
                                  ALU.add).then_inc(s_pos, 1)
                t.end()

            node_groups(dve, group)

            u = Steps(dve, s_tab)
            dve.wait_ge(s_wlo, 2 * E)
            dve.tensor_copy(filled_i[:, :], filled[0:1, :])
            u.did(dve.tensor_tensor(cnt[:, :], filled[0:1, :], region0[0:1, :], ALU.subtract))
            u.wait()
            u.did(dve.tensor_scalar(cnt_i[:, :], cnt[:, :], float(P - 1), None, ALU.add))
            u.wait()
            u.did(dve.tensor_scalar(nt_i[:, :], cnt_i[:, :], P.bit_length() - 1, None, ALU.logical_shift_right))
            u.wait()
            u.did(dve.tensor_copy(nt[:, :], nt_i[:, :]))
            u.wait()
            u.did(dve.tensor_tensor_scan(upto[:, :], one8[0:1, :], nt[:, :], 0.0, ALU.mult, ALU.add))
            u.wait()
            u.did(dve.tensor_tensor(ge[:, :, :], iota_j[:, :].unsqueeze(2).to_broadcast([1, TILES, E]),
                                    upto[:, :].unsqueeze(1).to_broadcast([1, TILES, E]), ALU.is_ge))
            u.wait()
            u.did(dve.tensor_tensor(gn[:, :, :], ge[:, :, :], nt[:, :].unsqueeze(1).to_broadcast([1, TILES, E]),
                                    ALU.mult))
            u.did(dve.tensor_reduce(tf[:, 0, :], ge[:, :, :], AX.X, ALU.add))
            u.wait()
            u.did(dve.tensor_reduce(tf[:, 1, :], gn[:, :, :], AX.X, ALU.add))
            dve.tensor_scalar(ti[:, 0, :], tf[:, 0, :], float(E - 1), None, ALU.min)
            u.wait()
            u.did(dve.tensor_tensor(tf[:, 2, :], iota_j[:, :], tf[:, 1, :], ALU.subtract))
            u.wait()
            u.did(dve.tensor_scalar(tf[:, 3, :], tf[:, 0, :], float(CAP), None, ALU.mult))
            u.wait()
            dve.scalar_tensor_tensor(ti[:, 1, :], tf[:, 2, :], float(P), tf[:, 3, :], ALU.mult, ALU.add)
            dve.tensor_copy(ti[:, 3, TILES - AHEAD:], ti[:, 0, TILES - AHEAD:])
            dve.scalar_tensor_tensor(ti[:, 3, 0:TILES - AHEAD], ti[:, 0, AHEAD:], float(E), ti[:, 0, 0:TILES - AHEAD],
                                     ALU.mult, ALU.add)
            dve.tensor_scalar(ti[:, 2, :], tf[:, 1, :], 2.0, None, ALU.max).then_inc(s_tables, 1)

            def expert(j):
                return dve.value_load(ti[0:1, 0, ds(j, 1)], min_val=0, max_val=E - 1)

            def add_bias1(j, s, e):
                dve.wait_ge(p_h, j + 1)
                if not isinstance(j, int) or j >= 2:
                    dve.wait_ge(p_hT, j - 1)
                dve.tensor_tensor(hb[:, s, :], bank[1 + s][:, :], b1bc[:, ds(e * HID, HID)],
                                  ALU.add).then_inc(p_bias, 1)
                slot = j % XR if isinstance(j, int) else j & (XR - 1)
                dve.tensor_copy(cwring[:, ds(j, 1)], xin_flat[:, ds(slot * ROW + CW + e, 1)]).then_inc(p_cw, 1)

            def add_bias2(j, s, e, first):
                dve.wait_ge(p_y, j + 1)
                if not first:
                    dve.wait_ge(p_add[s], 16 * half(j))
                dve.tensor_tensor(yb[:, s, :], bank[5 + s][:, 0:D], b2bc[:, ds(e * D, D)], ALU.add).then_inc(p_yb, 1)

            def x_low(j, s):
                dve.wait_ge(p_xhi, j + 1)
                dve.tensor_tensor(xTlo[:, s, :], bank[0][:, 0:D], xThi[:, s, :].bitcast(F32),
                                  ALU.subtract).then_inc(p_xlo, 1)

            def h_low(j, s):
                dve.wait_ge(p_hhi, j + 1)
                dve.tensor_tensor(hTlo[:, s, :], bank[3 + s][:, :], hThi[:, s, :].bitcast(F32),
                                  ALU.subtract).then_inc(p_hlo, 1)

            def half(j):
                return j // 2 if isinstance(j, int) else j >> 1

            dve.wait_ge(s_b1, 32)
            x_low(0, 0)
            add_bias1(0, 0, expert(0))
            x_low(1, 1)

            def step(j, s, e, load_next=True):
                add_bias1(j, s, e)
                start = isinstance(j, int) and j < 2
                e_back = None if start else expert(j - 2)
                if not (isinstance(j, int) and j + 1 >= TILES):
                    x_low(j + 1, 1 - s)
                if not start:
                    add_bias2(j - 2, s, e_back, isinstance(j, int) and j < 4)
                e_next = expert(j + 1) if load_next else None
                h_low(j - 1, 1 - s)
                return e_next

            e = step(1, 1, expert(1))
            e = step(2, 0, e)
            step(3, 1, e, False)
            with dve.Fori(2, (TILES - 1) // 2) as k:
                e = step(2 * k, 0, expert(2 * k))
                step(2 * k + 1, 1, e, False)
            for j in range((TILES - 1) // 2 * 2, TILES):
                step(j, j % 2, expert(j), False)
            e = expert(TILES - 2)
            add_bias2(TILES - 2, TILES % 2, e, False)
            e = expert(TILES - 1)
            h_low(TILES - 1, 1 - TILES % 2)
            add_bias2(TILES - 1, 1 - TILES % 2, e, False)

        @block.tensor
        def _(pe):
            pe.wait_ge(s_const, 19)
            pe.wait_ge(s_fold, N_FOLD)
            pe.wait_ge(s_bias, 32)

            def transpose_pair(to, src):
                for c in range(KC):
                    ins = pe.transpose(to[:, c * P:(c + 1) * P], src[:, c * P:(c + 1) * P], ident[:, :])
                return ins

            for c in range(KC):
                pe.matmul(bank[7][:, 0:D + 2 * H], ones32[:, :], wcat[:, c, :], start=c == 0, stop=c == KC - 1)
            for c in range(KC):
                ins = pe.matmul(bank[6][:, 0:E], ones32[:, :], gatew[:, c, :], start=c == 0, stop=c == KC - 1)
            ins.then_inc(s_sums, 1)

            def a_product(g, i):
                n_tile = GT * g + i + 1
                pe.wait_ge(a_turned, n_tile)
                if isinstance(g, int) and g == 0 and i == 0:
                    pe.wait_ge(s_centred, 2 * KC)
                if slot_used(g, i):
                    pe.wait_ge(a_out, n_tile - back(i))
                for c in range(KC):
                    ins = pe.matmul(bank[RING + i % RING][:, 0:D + 2 * H], turned[:, i % RING, c * P:(c + 1) * P],
                                    wcat[:, c, :], start=c == 0, stop=c == KC - 1)
                ins.then_inc(a_xt, 1)

            def a_group(g, s, h):
                for i in range(GT):
                    if i == 0:
                        pe.wait_ge(a_in[s], 16 * (h + 1))
                    if slot_used(g, i):
                        pe.wait_ge(a_turned, GT * g + i + 1 - back(i))
                    transpose_pair(bank[i % RING], xa[s][:, i, :]).then_inc(a_turn, 1)
                    if i:
                        a_product(g, i - 1)
                    elif not isinstance(g, int) or g > 0:
                        a_product(g - 1, GT - 1)

            node_groups(pe, a_group)
            a_product(LAST, GT - 1)

            def gate(g, i):
                pe.wait_ge(s_e2, GT * g + i + 1)
                for c in range(KC):
                    ins = pe.matmul(bank[5][:, i * E:(i + 1) * E], turned[:, i % RING, c * P:(c + 1) * P],
                                    gatew[:, c, :], start=c == 0, stop=c == KC - 1)
                ins.then_inc(s_gate, 1)

            def group(g):
                for i in range(GT):
                    pe.wait_ge(s_x2, GT * g + i + 1)
                    if slot_used(g, i):
                        pe.wait_ge(s_e2, GT * g + i + 1 - back(i))
                    transpose_pair(bank[i % RING], xg[:, i, :]).then_inc(s_t2, 1)
                    if i:
                        gate(g, i - 1)
                gate(g, GT - 1)
                pe.wait_ge(s_both, g + 1)
                r = bank[6][:, 0:GT * E].rearrange("p (t e) -> p t e", e=E)
                pe.matmul(r, upper[:, :], both16[:, :, :], start=True, stop=False)
                for i in range(GT - 1):
                    m = GT - 1 - i
                    pe.matmul(r[:, i + 1:GT, :], ones[:, :], both16[:, i:i + 1, :].to_broadcast([P, m, E]),
                              start=False, stop=i == GT - 2)
                for i in range(GT):
                    ins = pe.matmul(bank[6][:, 64:64 + E], ones[:, :], both16[:, i, :], start=i == 0, stop=i == GT - 1)
                ins.then_inc(s_ranks, 1)

            group(0)
            with pe.Fori(1, GROUPS) as g:
                group(g)

            def half(j):
                return j // 2 if isinstance(j, int) else j >> 1

            def turn_x(j, i):
                n_load = j // XR + 1 if isinstance(j, int) else (j >> 2) + 1
                pe.wait_ge(p_xin[i], 16 * n_load)
                if not isinstance(j, int) or j >= 1:
                    pe.wait_ge(p_xlo, j)
                transpose_pair(bank[0], xin[:, i, 0:D]).then_inc(p_xT, 1)

            def weights(of, base, start, width):
                return of[:, start:start + (E - 1) * WIDTH + width][:, ds(base, width)]

            def first_product(j, s, base, between=None):
                pe.wait_ge(p_xhi, j + 1)
                o = bank[1 + s][:, :]
                for c in range(KC):
                    lhs = xThi[:, s, c * P:(c + 1) * P]
                    pe.matmul(o, lhs, weights(w1hi, base, c * HID, HID), start=c == 0, stop=False)
                    pe.matmul(o, lhs, weights(w1lo, base, c * HID, HID), start=False, stop=False)
                result = between() if between else None
                pe.wait_ge(p_xlo, j + 1)
                for c in range(KC):
                    ins = pe.matmul(o, xTlo[:, s, c * P:(c + 1) * P], weights(w1hi, base, c * HID, HID), start=False,
                                    stop=c == KC - 1)
                ins.then_inc(p_h, 1)
                return result

            def turn_h(j, s):
                pe.wait_ge(p_gelu, j + 1)
                for c in range(HC):
                    ins = pe.transpose(bank[3 + s][:, c * P:(c + 1) * P], hb[:, s, c * P:(c + 1) * P], ident[:, :])
                ins.then_inc(p_hT, 1)

            def second_product(j, s, base):
                pe.wait_ge(p_hhi, j + 1)
                if not isinstance(j, int) or j >= 2:
                    pe.wait_ge(p_yb, j - 1)
                o = bank[5 + s][:, 0:D]
                for c in range(HC):
                    lhs = hThi[:, s, c * P:(c + 1) * P]
                    pe.matmul(o, lhs, weights(w2hi, base, c * D, D), start=c == 0, stop=False)
                    pe.matmul(o, lhs, weights(w2lo, base, c * D, D), start=False, stop=False)
                pe.wait_ge(p_hlo, j + 1)
                for c in range(HC):
                    ins = pe.matmul(o, hTlo[:, s, c * P:(c + 1) * P], weights(w2hi, base, c * D, D), start=False,
                                    stop=c == HC - 1)
                ins.then_inc(p_y, 1)

            def places(j):
                pair = pe.value_load(ti[0:1, 3, ds(j, 1)], min_val=0, max_val=E * E - 1)
                return (pair & (E - 1)) * WIDTH, ((pair >> (E.bit_length() - 1)) & (E - 1)) * WIDTH

            def place(j):
                return places(j)[0]

            turn_x(0, 0)
            first_product(0, 0, place(0))
            turn_x(1, 1)
            first_product(1, 1, place(1))
            turn_x(2, 2)
            turn_h(0, 0)
            first_product(2, 0, place(2))

            def step(j, i, now, end=False):
                s = i % 2
                on = not isinstance(j, int)
                here, ahead = now
                if on or j + AHEAD < TILES:
                    turn_x(j + AHEAD, (i + AHEAD) % XR)
                second_product(j, s, here)
                if on or j + 1 < TILES:
                    turn_h(j + 1, 1 - s)
                if on or j + AHEAD < TILES:
                    return first_product(j + AHEAD, 1 - s, ahead, None if end else lambda: places(j + 1))
                return places(j + 1) if j + 1 < TILES else None

            now = places(0)
            for j in range(XR):
                now = step(j, j, now, j == XR - 1)
            UNROLL = 2 * XR
            rounds = (TILES - AHEAD - XR) // UNROLL
            with pe.Fori(0, rounds) as k:
                now = places(UNROLL * k + XR)
                for i in range(UNROLL):
                    now = step(UNROLL * k + XR + i, i % XR, now, i == UNROLL - 1)
            start = UNROLL * rounds + XR
            now = places(start)
            for j in range(start, TILES):
                now = step(j, j % XR, now)


def kernel(x, src, dst, L0_gnn_weight, L0_gnn_attn_l, L0_gnn_attn_r, L0_ffn_gate_w, L0_ffn_gate_b, L0_ffn_W1,
           L0_ffn_b1, L0_ffn_W2, L0_ffn_b2):
    import numpy as np
    import concourse.bacc as bacc
    from concourse.bass_utils import run_bass_kernel_spmd

    x = np.asarray(x)
    n = x.shape[0]
    pad = padded_nodes(n) - n
    experts = np.shape(L0_ffn_gate_w)[1]

    def by_tile(index):
        a = np.pad(np.asarray(index)[:n], (0, pad)).reshape(-1, P, GT)
        return a.transpose(1, 0, 2)

    arrays = {
        "x": np.pad(x, ((0, pad), (0, 0))),
        "edges": np.ascontiguousarray(np.concatenate([by_tile(dst), by_tile(src)], axis=2)),
        "gnn_weight": np.ascontiguousarray(L0_gnn_weight),
        "attn_l": np.ascontiguousarray(L0_gnn_attn_l),
        "attn_r": np.ascontiguousarray(L0_gnn_attn_r),
        "gate_w": np.ascontiguousarray(L0_ffn_gate_w),
        "gate_b": np.ascontiguousarray(L0_ffn_gate_b),
        "w1": np.ascontiguousarray(L0_ffn_W1),
        "b1": np.ascontiguousarray(L0_ffn_b1),
        "w2": np.ascontiguousarray(L0_ffn_W2),
        "b2": np.ascontiguousarray(L0_ffn_b2),
    }
    nc = bacc.Bacc("TRN2", target_bir_lowering=False, num_devices=1)
    args = [nc.dram_tensor(k, a.shape, mybir.dt.from_np(a.dtype), kind="ExternalInput").ap()
            for k, a in arrays.items()]
    rows = n + pad + P * (1 + pieces(n, experts)[1])
    out = nc.dram_tensor("out", (rows, x.shape[1]), F32, kind="ExternalOutput").ap()
    gnn_moe(nc, n, *args, out)
    result = run_bass_kernel_spmd(nc, [arrays], core_ids=[0])
    return result.results[0]["out"][:n]
```
